# Optimizing a Trainium2 kernel written in Bass

```python
import numpy as np
import jax
import jax.numpy as jnp

def _softmax(x, axis=-1):
    return jax.nn.softmax(x, axis=axis)

def _gelu(x):
    return jax.nn.gelu(x, approximate=True)

def _silu(x):
    return jax.nn.silu(x)

def _sigmoid(x):
    return jax.nn.sigmoid(x)

def _layernorm(x, axis=-1, eps=1e-05):
    m = jnp.mean(x, axis=axis, keepdims=True)
    v = jnp.var(x, axis=axis, keepdims=True)
    return (x - m) / jnp.sqrt(v + eps)

def _scatter_add(tgt, idx, src, axis=0):
    return tgt.at[idx].add(src)

def _segment_sum(src, seg, n):
    return jax.ops.segment_sum(src, seg, n)
kernel_name = 'mk_recurrent_d2_jaxref_r4_45894d'

def setup_inputs(seed: int=0):
    np.random.seed(seed)
    _w = jnp.asarray

    def _L0_attn_setup():
        import jax, jax.numpy as jnp
        import numpy as np
        NUM_HEAD = 16
        D_Q = 128
        D_KV = 128
        ROPE_BASE = 10000.0

        def _cos_sin(seq_len, dim):
            pos = jnp.arange(seq_len, dtype=jnp.float32)[:, None]
            ids = jnp.arange(dim // 2, dtype=jnp.float32)
            theta = ROPE_BASE ** (-2.0 * ids) / (dim // 2)
            r = pos * theta[None, :]
            return (jnp.cos(r), jnp.sin(r))

        def _rope(x, cos, sin):
            b, s, d = x.shape
            xv = x.reshape(b, s, d // 2, 2)
            x0, x1 = (xv[..., 0], xv[..., 1])
            out = jnp.stack([x0 * cos - x1 * sin, x1 * cos + x0 * sin], axis=-1)
            return out.reshape(b, s, d)
        key = jax.random.key(seed)
        ks = jax.random.split(key, 10)
        d_model, d_q, d_kv = (256, D_Q, D_KV)
        b, s = (2, 512)
        w = lambda k, i, o: jax.random.normal(k, (i, o), dtype=jnp.float32) * 0.02
        return {'x': jax.random.normal(ks[0], (b, s, d_model), dtype=jnp.float32), 'Wd_q_w': w(ks[1], d_model, d_q), 'Wd_q_b': jnp.zeros((d_q,), jnp.float32), 'Wu_q_w': w(ks[2], d_q, d_model), 'Wu_q_b': jnp.zeros((d_model,), jnp.float32), 'Wq_r_w': w(ks[3], d_q, d_model), 'Wq_r_b': jnp.zeros((d_model,), jnp.float32), 'Wk_r_w': w(ks[4], d_model, d_model), 'Wk_r_b': jnp.zeros((d_model,), jnp.float32), 'Wd_kv_w': w(ks[5], d_model, d_kv), 'Wd_kv_b': jnp.zeros((d_kv,), jnp.float32), 'Wu_k_w': w(ks[6], d_kv, d_model), 'Wu_k_b': jnp.zeros((d_model,), jnp.float32), 'Wu_v_w': w(ks[7], d_kv, d_model), 'Wu_v_b': jnp.zeros((d_model,), jnp.float32), 'Wo_w': w(ks[8], d_model, d_model), 'Wo_b': jnp.zeros((d_model,), jnp.float32)}
    _L0_attn_in = _L0_attn_setup()

    def _L0_ffn_setup():
        import jax, jax.numpy as jnp
        import numpy as np
        B, S, D, E, H, K = (64, 512, 256, 32, 1024, 8)
        key = jax.random.key(seed)
        k0, k1, k2, k3 = jax.random.split(key, 4)
        x = jax.random.normal(k0, (B, S, D), jnp.float32)
        gate_w = jax.random.normal(k1, (E, D), jnp.float32) * (1.0 / np.sqrt(D))
        gate_b = jnp.zeros((E,), jnp.float32)
        w1 = jax.random.normal(k2, (E, D + 1, H), jnp.float32) * (1.0 / np.sqrt(D + 1))
        w2 = jax.random.normal(k3, (E, H + 1, D), jnp.float32) * (1.0 / np.sqrt(H + 1))
        return {'x': x, 'gate_w': gate_w, 'gate_b': gate_b, 'w1': w1, 'w2': w2}
    _L0_ffn_in = _L0_ffn_setup()

    def _L1_attn_setup():
        import jax, jax.numpy as jnp
        import numpy as np
        B_SZ, SEQ = (2, 512)
        D_MODEL, D_STATE, D_CONV = (256, 16, 4)
        D_INPUT, D_OUTPUT = (256, 256)
        D_INNER = 2 * D_MODEL
        DT_RANK = D_MODEL // 16
        key = jax.random.key(seed)
        ks = jax.random.split(key, 8)

        def rn(k, shape, scale):
            return (jax.random.normal(k, shape) * scale).astype(jnp.float32)
        return {'x': rn(ks[0], (B_SZ, SEQ, D_INPUT), 1.0), 'fc1_w': rn(ks[1], (D_MODEL, D_INPUT), D_INPUT ** (-0.5)), 'fc1_b': jnp.zeros((D_MODEL,), jnp.float32), 'in_proj_w': rn(ks[2], (2 * D_INNER, D_MODEL), D_MODEL ** (-0.5)), 'conv_w': rn(ks[3], (D_INNER, D_CONV), D_CONV ** (-0.5)), 'conv_b': jnp.zeros((D_INNER,), jnp.float32), 'x_proj_w': rn(ks[4], (DT_RANK + 2 * D_STATE, D_INNER), D_INNER ** (-0.5)), 'dt_proj_w': rn(ks[5], (D_INNER, DT_RANK), DT_RANK ** (-0.5)), 'dt_proj_b': jnp.full((D_INNER,), -4.6, jnp.float32), 'A_log': jnp.log(jnp.broadcast_to(jnp.arange(1, D_STATE + 1, dtype=jnp.float32), (D_INNER, D_STATE))), 'D': jnp.ones((D_INNER,), jnp.float32), 'out_proj_w': rn(ks[6], (D_MODEL, D_INNER), D_INNER ** (-0.5)), 'fc2_w': rn(ks[7], (D_OUTPUT, D_MODEL), D_MODEL ** (-0.5)), 'fc2_b': jnp.zeros((D_OUTPUT,), jnp.float32)}
    _L1_attn_in = _L1_attn_setup()

    def _L1_ffn_setup():
        import jax, jax.numpy as jnp
        import numpy as np
        DIM = 256
        HIDDEN = 768
        SCALE = 1.0 / 127.0

        def _dequant(w_int, dtype):
            return w_int.astype(dtype) * jnp.asarray(SCALE, dtype)
        key = jax.random.key(seed)
        k_x, k_g, k_u, k_d = jax.random.split(key, 4)
        x = jax.random.normal(k_x, (4, 512, DIM), dtype=jnp.float32)
        w_gate = jax.random.randint(k_g, (HIDDEN, DIM), -127, 128, dtype=jnp.int32)
        w_up = jax.random.randint(k_u, (HIDDEN, DIM), -127, 128, dtype=jnp.int32)
        w_down = jax.random.randint(k_d, (DIM, HIDDEN), -127, 128, dtype=jnp.int32)
        return {'x': x, 'w_gate': w_gate, 'w_up': w_up, 'w_down': w_down}
    _L1_ffn_in = _L1_ffn_setup()
    _d = {'L0_attn_x': _L0_attn_in['x'], 'L0_attn_Wd_q_w': _L0_attn_in['Wd_q_w'], 'L0_attn_Wd_q_b': _L0_attn_in['Wd_q_b'], 'L0_attn_Wu_q_w': _L0_attn_in['Wu_q_w'], 'L0_attn_Wu_q_b': _L0_attn_in['Wu_q_b'], 'L0_attn_Wq_r_w': _L0_attn_in['Wq_r_w'], 'L0_attn_Wq_r_b': _L0_attn_in['Wq_r_b'], 'L0_attn_Wk_r_w': _L0_attn_in['Wk_r_w'], 'L0_attn_Wk_r_b': _L0_attn_in['Wk_r_b'], 'L0_attn_Wd_kv_w': _L0_attn_in['Wd_kv_w'], 'L0_attn_Wd_kv_b': _L0_attn_in['Wd_kv_b'], 'L0_attn_Wu_k_w': _L0_attn_in['Wu_k_w'], 'L0_attn_Wu_k_b': _L0_attn_in['Wu_k_b'], 'L0_attn_Wu_v_w': _L0_attn_in['Wu_v_w'], 'L0_attn_Wu_v_b': _L0_attn_in['Wu_v_b'], 'L0_attn_Wo_w': _L0_attn_in['Wo_w'], 'L0_attn_Wo_b': _L0_attn_in['Wo_b'], 'L0_ffn_gate_w': _L0_ffn_in['gate_w'], 'L0_ffn_gate_b': _L0_ffn_in['gate_b'], 'L0_ffn_w1': _L0_ffn_in['w1'], 'L0_ffn_w2': _L0_ffn_in['w2'], 'L1_attn_fc1_w': _L1_attn_in['fc1_w'], 'L1_attn_fc1_b': _L1_attn_in['fc1_b'], 'L1_attn_in_proj_w': _L1_attn_in['in_proj_w'], 'L1_attn_conv_w': _L1_attn_in['conv_w'], 'L1_attn_conv_b': _L1_attn_in['conv_b'], 'L1_attn_x_proj_w': _L1_attn_in['x_proj_w'], 'L1_attn_dt_proj_w': _L1_attn_in['dt_proj_w'], 'L1_attn_dt_proj_b': _L1_attn_in['dt_proj_b'], 'L1_attn_A_log': _L1_attn_in['A_log'], 'L1_attn_D': _L1_attn_in['D'], 'L1_attn_out_proj_w': _L1_attn_in['out_proj_w'], 'L1_attn_fc2_w': _L1_attn_in['fc2_w'], 'L1_attn_fc2_b': _L1_attn_in['fc2_b'], 'L1_ffn_w_gate': _L1_ffn_in['w_gate'], 'L1_ffn_w_up': _L1_ffn_in['w_up'], 'L1_ffn_w_down': _L1_ffn_in['w_down']}
    _x0 = _d['L0_attn_x']
    _d['L0_attn_x'] = jax.random.normal(jax.random.fold_in(jax.random.key(seed), 1), (4, 2048, 256), dtype=_x0.dtype)
    del _x0
    return _d

def reference(L0_attn_x, L0_attn_Wd_q_w, L0_attn_Wd_q_b, L0_attn_Wu_q_w, L0_attn_Wu_q_b, L0_attn_Wq_r_w, L0_attn_Wq_r_b, L0_attn_Wk_r_w, L0_attn_Wk_r_b, L0_attn_Wd_kv_w, L0_attn_Wd_kv_b, L0_attn_Wu_k_w, L0_attn_Wu_k_b, L0_attn_Wu_v_w, L0_attn_Wu_v_b, L0_attn_Wo_w, L0_attn_Wo_b, L0_ffn_gate_w, L0_ffn_gate_b, L0_ffn_w1, L0_ffn_w2, L1_attn_fc1_w, L1_attn_fc1_b, L1_attn_in_proj_w, L1_attn_conv_w, L1_attn_conv_b, L1_attn_x_proj_w, L1_attn_dt_proj_w, L1_attn_dt_proj_b, L1_attn_A_log, L1_attn_D, L1_attn_out_proj_w, L1_attn_fc2_w, L1_attn_fc2_b, L1_ffn_w_gate, L1_ffn_w_up, L1_ffn_w_down):

    def _L0_attn_ref(x, Wd_q_w, Wd_q_b, Wu_q_w, Wu_q_b, Wq_r_w, Wq_r_b, Wk_r_w, Wk_r_b, Wd_kv_w, Wd_kv_b, Wu_k_w, Wu_k_b, Wu_v_w, Wu_v_b, Wo_w, Wo_b):
        import jax, jax.numpy as jnp
        import numpy as np
        NUM_HEAD = 16
        D_Q = 128
        D_KV = 128
        ROPE_BASE = 10000.0

        def _cos_sin(seq_len, dim):
            pos = jnp.arange(seq_len, dtype=jnp.float32)[:, None]
            ids = jnp.arange(dim // 2, dtype=jnp.float32)
            theta = ROPE_BASE ** (-2.0 * ids) / (dim // 2)
            r = pos * theta[None, :]
            return (jnp.cos(r), jnp.sin(r))

        def _rope(x, cos, sin):
            b, s, d = x.shape
            xv = x.reshape(b, s, d // 2, 2)
            x0, x1 = (xv[..., 0], xv[..., 1])
            out = jnp.stack([x0 * cos - x1 * sin, x1 * cos + x0 * sin], axis=-1)
            return out.reshape(b, s, d)
        b, s, d_model = x.shape
        h = NUM_HEAD
        hd = d_model // h
        scale = jnp.sqrt(jnp.float32(h + D_KV + D_Q))

        def heads(t):
            return t.reshape(b, s, h, hd).transpose(0, 2, 1, 3)
        cos, sin = _cos_sin(s, d_model)
        ct_q = x @ Wd_q_w + Wd_q_b
        qt_c = heads(ct_q @ Wu_q_w + Wu_q_b)
        qt_r = heads(_rope(ct_q @ Wq_r_w + Wq_r_b, cos, sin))
        query = qt_c + qt_r
        ct_kv = x @ Wd_kv_w + Wd_kv_b
        kt_c = heads(ct_kv @ Wu_k_w + Wu_k_b)
        kt_r = heads(_rope(x @ Wk_r_w + Wk_r_b, cos, sin))
        key = kt_c + kt_r
        value = heads(ct_kv @ Wu_v_w + Wu_v_b)
        attn = jnp.einsum('bhqd,bhkd->bhqk', query, key) / scale
        attn = jax.nn.softmax(attn, axis=-1)
        out = jnp.einsum('bhqk,bhkd->bhqd', attn, value)
        out = out.transpose(0, 2, 1, 3).reshape(b, s, d_model)
        return out @ Wo_w + Wo_b

    def _L0_ffn_ref(x, gate_w, gate_b, w1, w2):
        import jax, jax.numpy as jnp
        import numpy as np
        B, S, D, E, H, K = (64, 512, 256, 32, 1024, 8)
        b, s, d = x.shape
        logits = jnp.einsum('bsd,ed->bse', x, gate_w) + gate_b
        probs = jax.nn.softmax(logits, axis=-2)
        vals_t, idx_t = jax.lax.top_k(probs.transpose(0, 2, 1), K)
        vals = vals_t.transpose(0, 2, 1)
        idx = idx_t.transpose(0, 2, 1)
        flat_idx = idx.reshape(b, K * E)
        tok = jnp.take_along_axis(x, flat_idx[:, :, None], axis=1)
        tok = tok.reshape(b, K, E, d)
        merged = jnp.einsum('bked,bke->bed', tok, vals)
        ones = jnp.ones(merged.shape[:-1] + (1,), merged.dtype)
        h = jnp.einsum('bei,eih->beh', jnp.concatenate([merged, ones], -1), w1)
        h = jax.nn.gelu(h, approximate=False)
        o = jnp.einsum('bej,ejo->beo', jnp.concatenate([h, ones], -1), w2)
        out_tok = jnp.einsum('beo,bke->bkeo', o, vals).reshape(b, K * E, d)
        out = jnp.zeros_like(x).at[jnp.arange(b)[:, None], flat_idx].add(out_tok)
        return out

    def _L1_attn_ref(x, fc1_w, fc1_b, in_proj_w, conv_w, conv_b, x_proj_w, dt_proj_w, dt_proj_b, A_log, D, out_proj_w, fc2_w, fc2_b):
        import jax, jax.numpy as jnp
        import numpy as np
        B_SZ, SEQ = (2, 512)
        D_MODEL, D_STATE, D_CONV = (256, 16, 4)
        D_INPUT, D_OUTPUT = (256, 256)
        D_INNER = 2 * D_MODEL
        DT_RANK = D_MODEL // 16
        B, L, _ = x.shape
        d_inner, d_conv = conv_w.shape
        d_state = A_log.shape[1]
        dt_rank = dt_proj_w.shape[1]
        h = x @ fc1_w.T + fc1_b
        xz = h @ in_proj_w.T
        xc, z = jnp.split(xz, 2, axis=-1)
        xp = jnp.pad(xc, ((0, 0), (d_conv - 1, 0), (0, 0)))
        u = sum((xp[:, w:w + L, :] * conv_w[:, w] for w in range(d_conv))) + conv_b
        u = jax.nn.silu(u)
        x_dbl = u @ x_proj_w.T
        dt_low, Bm, Cm = jnp.split(x_dbl, [dt_rank, dt_rank + d_state], axis=-1)
        dt = jax.nn.softplus(dt_low @ dt_proj_w.T + dt_proj_b)
        A = -jnp.exp(A_log)

        def step(hstate, t):
            dt_t, B_t, C_t, u_t = t
            dA = jnp.exp(dt_t[..., None] * A)
            hstate = dA * hstate + (dt_t * u_t)[..., None] * B_t[:, None, :]
            y_t = jnp.einsum('bdn,bn->bd', hstate, C_t)
            return (hstate, y_t)
        h0 = jnp.zeros((B, d_inner, d_state), x.dtype)
        xs = (jnp.swapaxes(dt, 0, 1), jnp.swapaxes(Bm, 0, 1), jnp.swapaxes(Cm, 0, 1), jnp.swapaxes(u, 0, 1))
        _, ys = jax.lax.scan(step, h0, xs)
        y = jnp.swapaxes(ys, 0, 1) + u * D
        y = y * jax.nn.silu(z)
        out = y @ out_proj_w.T
        return out @ fc2_w.T + fc2_b

    def _L1_ffn_ref(x, w_gate, w_up, w_down):
        import jax, jax.numpy as jnp
        import numpy as np
        DIM = 256
        HIDDEN = 768
        SCALE = 1.0 / 127.0

        def _dequant(w_int, dtype):
            return w_int.astype(dtype) * jnp.asarray(SCALE, dtype)
        wg = _dequant(w_gate, x.dtype)
        wu = _dequant(w_up, x.dtype)
        wd = _dequant(w_down, x.dtype)
        gate = jnp.einsum('bsd,hd->bsh', x, wg)
        up = jnp.einsum('bsd,hd->bsh', x, wu)
        h = jax.nn.silu(gate) * up
        return jnp.einsum('bsh,dh->bsd', h, wd)
    x = L0_attn_x
    xn = _layernorm(x, axis=-1)
    s = _L0_attn_ref(xn, L0_attn_Wd_q_w, L0_attn_Wd_q_b, L0_attn_Wu_q_w, L0_attn_Wu_q_b, L0_attn_Wq_r_w, L0_attn_Wq_r_b, L0_attn_Wk_r_w, L0_attn_Wk_r_b, L0_attn_Wd_kv_w, L0_attn_Wd_kv_b, L0_attn_Wu_k_w, L0_attn_Wu_k_b, L0_attn_Wu_v_w, L0_attn_Wu_v_b, L0_attn_Wo_w, L0_attn_Wo_b)
    g = _silu(_L0_ffn_ref(xn, L0_ffn_gate_w, L0_ffn_gate_b, L0_ffn_w1, L0_ffn_w2))
    x = x + s * g
    xn = _layernorm(x, axis=-1)
    s = _L1_attn_ref(xn, L1_attn_fc1_w, L1_attn_fc1_b, L1_attn_in_proj_w, L1_attn_conv_w, L1_attn_conv_b, L1_attn_x_proj_w, L1_attn_dt_proj_w, L1_attn_dt_proj_b, L1_attn_A_log, L1_attn_D, L1_attn_out_proj_w, L1_attn_fc2_w, L1_attn_fc2_b)
    g = _silu(_L1_ffn_ref(xn, L1_ffn_w_gate, L1_ffn_w_up, L1_ffn_w_down))
    x = x + s * g
    return x

_drawn_inputs = setup_inputs


def setup_inputs(seed=0):
    import zlib

    import numpy as np

    out = dict(_drawn_inputs(seed))
    spreads = {'L0_attn_Wd_q_b': (0.0, 0.8),
     'L0_attn_Wu_q_b': (0.0, 0.8),
     'L0_attn_Wq_r_b': (0.0, 0.8),
     'L0_attn_Wk_r_b': (0.0, 0.8),
     'L0_attn_Wd_kv_b': (0.0, 0.8),
     'L0_attn_Wu_k_b': (0.0, 0.8),
     'L0_attn_Wu_v_b': (0.0, 0.8),
     'L0_attn_Wo_b': (0.0, 0.8),
     'L0_ffn_gate_b': (0.0, 0.8),
     'L1_attn_fc1_b': (0.0, 0.1),
     'L1_attn_conv_b': (0.0, 0.1),
     'L1_attn_dt_proj_b': (-4.599999904632568, 0.2),
     'L1_attn_D': (1.0, 0.2),
     'L1_attn_fc2_b': (0.0, 0.1)}
    factors = {'L0_attn_Wd_q_w': 8.0,
     'L0_attn_Wu_q_w': 8.0,
     'L0_attn_Wq_r_w': 8.0,
     'L0_attn_Wk_r_w': 8.0,
     'L0_attn_Wd_kv_w': 8.0,
     'L0_attn_Wu_k_w': 8.0,
     'L0_attn_Wu_v_w': 8.0,
     'L0_attn_Wo_w': 8.0,
     'L0_ffn_gate_w': 8.0,
     'L0_ffn_w1': 7.4,
     'L0_ffn_w2': 7.247}
    for name, (base, spread) in spreads.items():
        noise = np.random.default_rng([zlib.crc32(name.encode()), seed]).standard_normal(out[name].shape)
        drawn = base * np.exp(spread * noise) if base else spread * noise
        out[name] = jnp.asarray(drawn.astype(out[name].dtype))
    for name, factor in factors.items():
        out[name] = (out[name] * factor).astype(out[name].dtype)
    return out
```

```python
from contextlib import ExitStack

import numpy as np

import concourse.bass as bass
from concourse import mybir

F32 = mybir.dt.float32
BF16 = mybir.dt.bfloat16
U32 = mybir.dt.uint32
I32 = mybir.dt.int32
ALU = mybir.AluOpType
ACT = mybir.ActivationFunctionType
AX = mybir.AxisListType

B, S, D = 4, 2048, 256
P = 128
TT = 512
NT = B * S // TT
NC = S // TT
KD = D // P
NH, HD = 16, 16
HG = 4
NE, TOPK = 32, 8
NS = B * NE * TOPK
SB = NE * TOPK
HID = 1024
VW = HD + 1
EPS = 1e-5
ATT = 1.0 / float((16 + 128 + 128) ** 0.5)
DI = 512
CB = DI // P
NST = 16
RK = 16
FH = 768
FB = FH // P


def wait(eng, sem, value):
    if not isinstance(value, int) or value > 0:
        eng.wait_ge(sem, value)


def steps(eng, step, head, pairs, total):
    for t in range(head):
        step(t, t % 2, t // 2)
    with eng.Fori(0, pairs) as j:
        for p in range(2):
            step(j * 2 + (head + p), p, j + head // 2)
    for t in range(head + 2 * pairs, total):
        step(t, t % 2, t // 2)


def tokens_stage(nc, ins, scr):
    with ExitStack() as ctx:
        sb = lambda n, s, d=F32: ctx.enter_context(nc.sbuf_tensor("t_" + n, s, d))
        ps = lambda n, s, d=F32: ctx.enter_context(nc.psum_tensor("t_" + n, s, d))
        sem = lambda n: ctx.enter_context(nc.semaphore("t_" + n))
        two = range(2)

        ident = sb("ident", [P, P])
        w_dkv = sb("w_dkv", [P, KD, P])
        w_kr = sb("w_kr", [P, KD, D])
        w_uk = sb("w_uk", [P, D])
        w_uv = sb("w_uv", [P, D])
        w_gate = sb("w_gate", [P, KD, NE])
        b_dkv = sb("b_dkv", [P, 1])
        b_kr = sb("b_kr", [P, 2])
        b_uk = sb("b_uk", [P, 2])
        b_uv = sb("b_uv", [P, D])
        b_gate = sb("b_gate", [NE, 1])
        eps = sb("eps", [P, 1])
        spare = sb("spare", [P, 1])
        xb = [sb(f"xb{p}", [P, 4, D]) for p in two]
        cs = [sb(f"cs{p}", [P, 2, TT]) for p in two]
        stats = [sb(f"stats{p}", [P, 4, 6]) for p in two]
        mv = [sb(f"mv{p}", [P, 4, 2]) for p in two]
        rstd = [sb(f"rstd{p}", [P, 4]) for p in two]
        std = [sb(f"std{p}", [P, 4]) for p in two]
        xn = [sb(f"xn{p}", [P, 4, D]) for p in two]
        xnT = [sb(f"xnT{p}", [P, KD, TT]) for p in two]
        ckvT = [sb(f"ckvT{p}", [P, TT]) for p in two]
        lgs = [sb(f"lgs{p}", [NE, TT]) for p in two]
        rot = [sb(f"rot{p}", [P, 4, TT]) for p in two]
        k32 = [sb(f"k32{p}", [P, 2, TT]) for p in two]
        rest = [sb(f"rest{p}", [P, 2, TT]) for p in two]
        kp = [sb(f"kp{p}", [P, 3, 2, TT], BF16) for p in two]
        vo = [sb(f"vo{p}", [P, HG, 4, 4, VW]) for p in two]

        p_t = ps("p_t", [P, KD, TT])
        p_lg = ps("p_lg", [P, TT])
        p_ck = ps("p_ck", [P, TT])
        p_kr = ps("p_kr", [P, 2, TT])
        p_kc = ps("p_kc", [P, 2, TT])

        consts = sem("consts")
        x_in = [sem(f"x_in{p}") for p in two]
        cs_in = [sem(f"cs_in{p}") for p in two]
        stored = [sem(f"stored{p}") for p in two]
        ones_set = sem("ones_set")
        eps_set = sem("eps_set")
        stats_ok, aggr_ok, std_ok, rstd_ok, xn_ok = (sem(n) for n in ("stats_ok", "aggr_ok", "std_ok", "rstd_ok", "xn_ok"))
        tr_ok, xnT_ok, ck_ok, kr_ok, ckvT_ok, lg_ok, kc_ok, v_ok = (
            sem(n) for n in ("tr_ok", "xnT_ok", "ck_ok", "kr_ok", "ckvT_ok", "lg_ok", "kc_ok", "v_ok"))
        vo_ok, rot_ok, ksum_ok, k32_ok, hi_ok, r1_ok, mid_ok, kp_ok = (
            sem(n) for n in ("vo_ok", "rot_ok", "ksum_ok", "k32_ok", "hi_ok", "r1_ok", "mid_ok", "kp_ok"))
        N_CONST = 12

        with nc.Block() as block:
            @block.sync
            def _(eng):
                for dst, src in ((ident[:, :], ins["ident"]),
                                 (w_dkv[:, :, :], ins["Wd_kv"].rearrange("(k p) m -> p k m", p=P)),
                                 (w_kr[:, :, :], ins["Wk_r"].rearrange("(k p) m -> p k m", p=P)),
                                 (w_uk[:, :], ins["Wu_k"]), (w_uv[:, :], ins["Wu_v"]),
                                 (w_gate[:, :, :], ins["gateT"].rearrange("(k p) m -> p k m", p=P)),
                                 (b_dkv[:, :], ins["b_dkv"]), (b_kr[:, :], ins["b_kr"]),
                                 (b_uk[:, :], ins["b_uk"]), (b_gate[:, :], ins["b_gate"]),
                                 (b_uv[:, :], ins["b_uv"].partition_broadcast(P))):
                    eng.dma_start(dst, src).then_inc(consts, 16)
                eng.dma_start(scr["x1"].rearrange("(p a) d -> p (a d)", p=P),
                              ins["x"].rearrange("(p a) d -> p (a d)", p=P)).then_inc(consts, 16)

                def load(t, p, h):
                    wait(eng, xn_ok, t - 1)
                    eng.dma_start(xb[p][:, :, :], ins["x"][bass.ds(t * TT, TT), :].rearrange("(a p) d -> p a d", p=P))\
                       .then_inc(x_in[p], 16)

                def step(t, p, h):
                    if not (isinstance(t, int) and t >= NT):
                        load(t, p, h)
                        wait(eng, ksum_ok, t - 1)
                        eng.dma_start(cs[p][:, :, :], ins["cs_tiles"][bass.ds(t * P, P), :, :]).then_inc(cs_in[p], 16)
                    if isinstance(t, int) and t < 2:
                        return
                    r = t - 2
                    eng.wait_ge(kp_ok, r + 1)
                    for g in range(6):
                        part, eo = divmod(g, 2)
                        dst = scr["kp"][bass.ds(r * (HG * 48), HG * 48), :].rearrange(
                            "(a q z) t -> a q (z t)", a=HG, q=6)[:, g, :].rearrange("a (z t) -> a z t", t=TT)
                        eng.dma_start(dst, kp[p][:, part, eo, :]).then_inc(stored[p], 16)
                    eng.wait_ge(vo_ok, r + 1)
                    eng.dma_start(scr["vp"][bass.ds(r * HG, HG), :, :].rearrange("a p n -> p a n"),
                                  vo[p][:, :, :, :, :].rearrange("p a b c d -> p a (b c d)")).then_inc(stored[p], 16)
                    eng.wait_ge(lg_ok, r + 1)
                    eng.dma_start(scr["lg"][bass.ds(r * NE, NE), :], lgs[p][:, :]).then_inc(stored[p], 16)

                steps(eng, step, 2, 7, NT + 2)
                for p in two:
                    eng.wait_ge(stored[p], 16 * 8 * (NT // 2))

            @block.vector
            def _(eng):
                eng.memset(eps[:, :], EPS).then_inc(eps_set, 1)
                eng.wait_ge(consts, 16 * N_CONST)

                def norm(t, p, h):
                    eng.wait_ge(x_in[p], h * 16 + 16)
                    for a in range(4):
                        i = eng.bn_stats(stats[p][:, a, :], xb[p][:, a, :])
                    i.then_inc(stats_ok, 1)
                    eng.wait_ge(stats_ok, t + 1)
                    eng.memset(spare[:, :], 0.0)
                    for a in range(4):
                        i = eng.bn_aggr(mv[p][:, a, :], stats[p][:, a, :])
                    i.then_inc(aggr_ok, 1)
                    eng.wait_ge(std_ok, t + 1)
                    eng.reciprocal(rstd[p][:, :], std[p][:, :]).then_inc(rstd_ok, 1)
                    eng.wait_ge(rstd_ok, t + 1)
                    wait(eng, tr_ok, t - 1)
                    for a in range(4):
                        i = eng.tensor_scalar(xn[p][:, a, :], xb[p][:, a, :], mv[p][:, a, 0:1], rstd[p][:, a:a + 1],
                                              ALU.subtract, ALU.mult)
                    i.then_inc(xn_ok, 1)

                def keys(r, p, h):
                    eng.wait_ge(v_ok, r + 1)
                    wait(eng, stored[p], h * 128)
                    for a in range(4):
                        i = eng.tensor_tensor(vo[p][:, :, a, :, 0:HD],
                                              p_t[:, :, :].rearrange("p k n -> p (k n)")[:, a * D:(a + 1) * D]
                                              .rearrange("p (g h d) -> p g h d", g=HG, h=4),
                                              b_uv[:, :].rearrange("p (g h d) -> p g h d", g=HG, h=4), ALU.add)
                    i.then_inc(vo_ok, 1)
                    eng.wait_ge(cs_in[p], h * 16 + 16)
                    wait(eng, k32_ok, r - 1)
                    for n, (eo, tri) in enumerate(((0, 0), (1, 1), (1, 0), (0, 1))):
                        i = eng.scalar_tensor_tensor(rot[p][:, n, :], p_kr[:, eo, :], b_kr[:, eo:eo + 1],
                                                     cs[p][:, tri, :], ALU.add, ALU.mult)
                    i.then_inc(rot_ok, 1)
                    eng.wait_ge(rot_ok, r + 1)
                    wait(eng, r1_ok, r - 1)
                    for eo in range(2):
                        i = eng.scalar_tensor_tensor(k32[p][:, eo, :], p_kc[:, eo, :], b_uk[:, eo:eo + 1],
                                                     rot[p][:, 2 * eo, :], ALU.add, ALU.add)
                    i.then_inc(ksum_ok, 1)

                def step(t, p, h):
                    if not (isinstance(t, int) and t >= NT):
                        norm(t, p, h)
                    if not (isinstance(t, int) and t < 1):
                        keys(t - 1, 1 - p, h if p else h - 1)

                steps(eng, step, 2, 7, NT + 1)

            @block.scalar
            def _(eng):
                eng.wait_ge(eps_set, 1)
                eng.wait_ge(consts, 16 * N_CONST)

                def front(t, p, h):
                    eng.wait_ge(aggr_ok, t + 1)
                    eng.activation(std[p][:, :], mv[p][:, :, 1], ACT.Sqrt, bias=eps[:, 0:1]).then_inc(std_ok, 1)
                    eng.wait_ge(tr_ok, t + 1)
                    eng.activation(xnT[p][:, :, :], p_t[:, :, :], ACT.Copy).then_inc(xnT_ok, 1)
                    eng.wait_ge(ck_ok, t + 1)
                    eng.activation(ckvT[p][:, :], p_ck[:, :], ACT.Identity, bias=b_dkv[:, 0:1]).then_inc(ckvT_ok, 1)
                    wait(eng, stored[p], h * 128)
                    eng.activation(lgs[p][:, :], p_lg[0:NE, :], ACT.Identity, bias=b_gate[:, 0:1]).then_inc(lg_ok, 1)

                def split(r, p, h):
                    eng.wait_ge(k32_ok, r + 1)
                    wait(eng, stored[p], h * 128)
                    eng.activation(kp[p][:, 0, :, :], k32[p][:, :, :], ACT.Copy).then_inc(hi_ok, 1)
                    eng.wait_ge(r1_ok, r + 1)
                    eng.activation(kp[p][:, 1, :, :], rest[p][:, :, :], ACT.Copy).then_inc(mid_ok, 1)

                def step(t, p, h):
                    if not (isinstance(t, int) and t >= NT):
                        front(t, p, h)
                    if not (isinstance(t, int) and t < 1):
                        split(t - 1, 1 - p, h if p else h - 1)

                steps(eng, step, 2, 7, NT + 1)

            @block.gpsimd
            def _(eng):
                for p in two:
                    i = eng.memset(vo[p][:, :, :, :, HD:VW], 1.0)
                i.then_inc(ones_set, 1)
                eng.wait_ge(ones_set, 1)

                def step(r, p, h):
                    eng.wait_ge(ksum_ok, r + 1)
                    eng.tensor_tensor(k32[p][:, 0, :], k32[p][:, 0, :], rot[p][:, 1, :], ALU.subtract)
                    eng.tensor_tensor(k32[p][:, 1, :], k32[p][:, 1, :], rot[p][:, 3, :], ALU.add).then_inc(k32_ok, 1)
                    eng.wait_ge(hi_ok, r + 1)
                    eng.wait_ge(k32_ok, r + 1)
                    eng.tensor_tensor(rest[p][:, :, :], k32[p][:, :, :], kp[p][:, 0, :, :], ALU.subtract).then_inc(r1_ok, 1)
                    eng.wait_ge(mid_ok, r + 1)
                    eng.wait_ge(r1_ok, r + 1)
                    eng.tensor_tensor(kp[p][:, 2, :, :], rest[p][:, :, :], kp[p][:, 1, :, :], ALU.subtract).then_inc(kp_ok, 1)

                steps(eng, step, 2, 7, NT)

            @block.tensor
            def _(eng):
                eng.wait_ge(consts, 16 * N_CONST)

                def step(t, p, h):
                    eng.wait_ge(xn_ok, t + 1)
                    wait(eng, vo_ok, t)
                    for k in range(KD):
                        for a in range(4):
                            i = eng.transpose(p_t[:, k, a * P:(a + 1) * P], xn[p][:, a, k * P:(k + 1) * P], ident[:, :])
                    i.then_inc(tr_ok, 1)
                    eng.wait_ge(xnT_ok, t + 1)
                    wait(eng, lg_ok, t)
                    for k in range(KD):
                        eng.matmul(p_lg[0:NE, :], w_gate[:, k, :], xnT[p][:, k, :], start=k == 0, stop=k == KD - 1)
                    for k in range(KD):
                        i = eng.matmul(p_ck[:, :], w_dkv[:, k, :], xnT[p][:, k, :], start=k == 0, stop=k == KD - 1)
                    i.then_inc(ck_ok, 1)
                    wait(eng, ksum_ok, t)
                    for eo in range(2):
                        for k in range(KD):
                            i = eng.matmul(p_kr[:, eo, :], w_kr[:, k, eo * P:(eo + 1) * P], xnT[p][:, k, :],
                                           start=k == 0, stop=k == KD - 1)
                    i.then_inc(kr_ok, 1)
                    eng.wait_ge(ckvT_ok, t + 1)
                    for eo in range(2):
                        i = eng.matmul(p_kc[:, eo, :], w_uk[:, eo * P:(eo + 1) * P], ckvT[p][:, :], start=True, stop=True)
                    i.then_inc(kc_ok, 1)
                    for a in range(4):
                        i = eng.matmul(p_t[:, a // 2, (a % 2) * D:(a % 2 + 1) * D], ckvT[p][:, a * P:(a + 1) * P], w_uv[:, :],
                                       start=True, stop=True)
                    i.then_inc(v_ok, 1)

                steps(eng, step, 2, 7, NT)


def routing_stage(nc, ins, scr, keep):
    with ExitStack() as ctx:
        sb = lambda n, s, d=F32: ctx.enter_context(nc.sbuf_tensor("r_" + n, s, d))
        ps = lambda n, s, d=F32: ctx.enter_context(nc.psum_tensor("r_" + n, s, d))
        sem = lambda n: ctx.enter_context(nc.semaphore("r_" + n))
        K8 = TOPK
        w_dq = sb("w_dq", [P, KD, P])
        w_uq = sb("w_uq", [P, D])
        w_qr = sb("w_qr", [P, D])
        b_dq = sb("b_dq", [P, 1])
        b_uq = sb("b_uq", [P, D])
        b_qr = sb("b_qr", [P, D])
        first = sb("first", [P, 1])
        eps = sb("eps", [P, 1])
        lg = sb("lg", [P, S])
        ex = sb("ex", [P, S])
        m8 = sb("m8", [P, K8])
        nmax = sb("nmax", [P, 1])
        e8 = sb("e8", [P, K8])
        total = sb("total", [P, 1])
        rtotal = sb("rtotal", [P, 1])
        i8 = sb("i8", [P, K8], U32)
        g8 = sb("g8", [P, K8], U32)
        csg = sb("csg", [P, K8, D])
        stats = sb("stats", [P, K8, 6])
        mv = sb("mv", [P, K8, 2])
        std = sb("std", [P, K8])
        rstd = sb("rstd", [P, K8])
        xg_n = sb("xg_n", [P, K8, D])
        xgT = sb("xgT", [P, KD, NS])
        ctqT = sb("ctqT", [P, NS])
        merged = sb("merged", [P, D])
        qr = sb("qr", [P, K8, D])
        qs = sb("qs", [P, K8, D])
        t1 = [sb(f"t1{eo}", [P, K8, P]) for eo in range(2)]
        t2 = [sb(f"t2{eo}", [P, K8, P]) for eo in range(2)]
        qT = sb("qT", [P, 2, NS])
        qrest = sb("qrest", [P, 2, NS])
        qp = sb("qp", [P, 3, 2, NS], BF16)
        ident, xg, vals, gf, mergedT = (keep[n] for n in ("ident", "xg", "vals", "gf", "mergedT"))

        p_a = ps("p_a", [P, 4, TT])
        p_b = ps("p_b", [P, 4, TT])

        consts, lg_in, eps_set = sem("consts"), sem("lg_in"), sem("eps_set")
        dve, act, pe = sem("dve"), sem("act"), sem("pe")
        rows_in, cs_in, idx_out, q_out = sem("rows_in"), sem("cs_in"), sem("idx_out"), sem("q_out")

        V_TOP, V_NMAX, V_IDX, V_GLOBAL, V_STATS, V_AGGR, V_RTOTAL, V_VALS, V_RSTD, V_ROWS = range(1, 11)
        V_MERGED = V_ROWS + K8
        (V_QC0, V_QR0, V_QC1, V_QR1, V_ROT, V_ROT2, V_ROT3, V_ROT4, V_QSUM, V_R1, V_LO) = range(V_MERGED + 1, V_MERGED + 12)
        (A_E8, A_EX, A_STD, A_XGT0, A_XGT1, A_CTQ, A_MT, A_QT0, A_QT1, A_HI, A_MID) = range(1, 12)
        (T_XGT0, T_XGT1, T_CTQ, T_MT, T_Q0, T_Q1, T_QT0, T_QT1) = range(1, 9)

        with nc.Block() as block:
            @block.sync
            def _(eng):
                for b in range(B):
                    eng.dma_start(lg[b * NE:(b + 1) * NE, :].rearrange("e (c t) -> e c t", c=NC),
                                  scr["lg"].rearrange("(b c e) t -> b e c t", b=B, c=NC)[b]).then_inc(lg_in, 16)
                for dst, src in ((ident[:, :], ins["ident"]),
                                 (w_dq[:, :, :], ins["Wd_q"].rearrange("(k p) m -> p k m", p=P)),
                                 (w_uq[:, :], ins["Wu_q"]), (w_qr[:, :], ins["Wq_r"]), (b_dq[:, :], ins["b_dq"]),
                                 (b_uq[:, :], ins["b_uq"].partition_broadcast(P)),
                                 (b_qr[:, :], ins["b_qr"].partition_broadcast(P)),
                                 (first[:, :], ins["first"])):
                    eng.dma_start(dst, src).then_inc(consts, 16)
                eng.wait_ge(dve, V_GLOBAL)
                eng.dma_start(scr["rows"], gf[:, :]).then_inc(idx_out, 16)
                eng.wait_ge(dve, V_LO)
                for g in range(6):
                    for b in range(B):
                        eng.dma_start(scr["qp"].rearrange("b a (q z) t -> b q a z t", q=6)[b, g],
                                      qp[:, g // 2, g % 2, b * SB:(b + 1) * SB]).then_inc(q_out, 16)
                eng.wait_ge(idx_out, 16)
                eng.wait_ge(q_out, 16 * 6 * B)

            @block.gpsimd
            def _(eng):
                eng.memset(eps[:, :], EPS).then_inc(eps_set, 1)
                eng.wait_ge(dve, V_GLOBAL)
                for k in range(K8):
                    eng.indirect_dma_start(xg[:, k, :], None, ins["x"],
                                           bass.IndirectOffsetOnAxis(g8[:, k:k + 1], 0)).then_inc(rows_in, 16)
                for k in range(K8):
                    eng.indirect_dma_start(csg[:, k, :], None, ins["cs_rows"],
                                           bass.IndirectOffsetOnAxis(i8[:, k:k + 1], 0)).then_inc(cs_in, 16)
                eng.wait_ge(rows_in, 16 * K8)
                eng.wait_ge(cs_in, 16 * K8)

            @block.vector
            def _(eng):
                eng.wait_ge(lg_in, 16 * B)
                eng.max(m8[:, :], lg[:, :]).then_inc(dve, 1)
                eng.wait_ge(dve, V_TOP)
                eng.tensor_scalar(nmax[:, :], m8[:, 0:1], -1.0, None, ALU.mult).then_inc(dve, 1)
                eng.max_index(i8[:, :], m8[:, :], lg[:, :]).then_inc(dve, 1)
                eng.wait_ge(consts, 16 * 8)
                eng.wait_ge(dve, V_IDX)
                eng.tensor_scalar(g8[:, :], i8[:, :], first[:, 0:1], None, ALU.add)
                eng.tensor_scalar(gf[:, :], i8[:, :], first[:, 0:1], None, ALU.add).then_inc(dve, 1)
                eng.wait_ge(rows_in, 16 * K8)
                for k in range(K8):
                    i = eng.bn_stats(stats[:, k, :], xg[:, k, :])
                i.then_inc(dve, 1)
                eng.wait_ge(dve, V_STATS)
                for k in range(K8):
                    i = eng.bn_aggr(mv[:, k, :], stats[:, k, :])
                i.then_inc(dve, 1)
                eng.wait_ge(act, A_EX)
                eng.reciprocal(rtotal[:, :], total[:, :]).then_inc(dve, 1)
                eng.wait_ge(dve, V_RTOTAL)
                eng.tensor_scalar(vals[:, :], e8[:, :], rtotal[:, 0:1], None, ALU.mult).then_inc(dve, 1)
                eng.wait_ge(act, A_STD)
                eng.reciprocal(rstd[:, :], std[:, :]).then_inc(dve, 1)
                eng.wait_ge(dve, V_RSTD)
                for k in range(K8):
                    i = eng.tensor_scalar(xg_n[:, k, :], xg[:, k, :], mv[:, k, 0:1], rstd[:, k:k + 1], ALU.subtract, ALU.mult)
                i.then_inc(dve, 1)
                eng.wait_ge(dve, V_ROWS)
                eng.tensor_scalar(merged[:, :], xg_n[:, 0, :], vals[:, 0:1], None, ALU.mult).then_inc(dve, 1)
                for k in range(1, K8):
                    eng.wait_ge(dve, V_ROWS + k)
                    eng.scalar_tensor_tensor(merged[:, :], xg_n[:, k, :], vals[:, k:k + 1], merged[:, :], ALU.mult, ALU.add)\
                       .then_inc(dve, 1)
                for half in range(2):
                    eng.wait_ge(pe, (T_Q0, T_Q1)[half])
                    kk = slice(4 * half, 4 * half + 4)
                    eng.tensor_tensor(qs[:, kk, :], p_a[:, :, 0:D], b_uq[:, :].unsqueeze(1).broadcast_to([P, 4, D]), ALU.add)\
                       .then_inc(dve, 1)
                    eng.tensor_tensor(qr[:, kk, :], p_b[:, :, 0:D], b_qr[:, :].unsqueeze(1).broadcast_to([P, 4, D]), ALU.add)\
                       .then_inc(dve, 1)
                eng.wait_ge(cs_in, 16 * K8)
                eng.wait_ge(dve, V_QR1)
                for eo in range(2):
                    mine, other = qr[:, :, eo * P:(eo + 1) * P], qr[:, :, (1 - eo) * P:(2 - eo) * P]
                    eng.tensor_tensor(t1[eo][:, :, :], mine, csg[:, :, 0:P], ALU.mult)
                    eng.tensor_tensor(t2[eo][:, :, :], other, csg[:, :, P:2 * P], ALU.mult).then_inc(dve, 1)
                    eng.wait_ge(dve, (V_ROT, V_ROT3)[eo])
                    eng.tensor_tensor(t1[eo][:, :, :], t1[eo][:, :, :], t2[eo][:, :, :], (ALU.subtract, ALU.add)[eo]).then_inc(dve, 1)
                    eng.wait_ge(dve, (V_ROT2, V_ROT4)[eo])
                    i = eng.tensor_tensor(qs[:, :, eo * P:(eo + 1) * P], qs[:, :, eo * P:(eo + 1) * P], t1[eo][:, :, :], ALU.add)
                i.then_inc(dve, 1)
                eng.wait_ge(act, A_HI)
                eng.tensor_tensor(qrest[:, :, :], qT[:, :, :], qp[:, 0, :, :], ALU.subtract).then_inc(dve, 1)
                eng.wait_ge(act, A_MID)
                eng.tensor_tensor(qp[:, 2, :, :], qrest[:, :, :], qp[:, 1, :, :], ALU.subtract).then_inc(dve, 1)

            @block.scalar
            def _(eng):
                eng.wait_ge(dve, V_NMAX)
                eng.activation(e8[:, :], m8[:, :], ACT.Exp, bias=nmax[:, 0:1]).then_inc(act, 1)
                eng.activation(ex[:, :], lg[:, :], ACT.Exp, bias=nmax[:, 0:1], accum_out=total[:, 0:1]).then_inc(act, 1)
                eng.wait_ge(dve, V_AGGR)
                eng.wait_ge(eps_set, 1)
                eng.activation(std[:, :], mv[:, :, 1], ACT.Sqrt, bias=eps[:, 0:1]).then_inc(act, 1)
                for half in range(2):
                    eng.wait_ge(pe, (T_XGT0, T_XGT1)[half])
                    for k in range(KD):
                        i = eng.activation(xgT[:, k, half * TT:(half + 1) * TT], (p_a, p_b)[half][:, k, :], ACT.Copy)
                    i.then_inc(act, 1)
                eng.wait_ge(pe, T_CTQ)
                eng.activation(ctqT[:, :], p_a[:, 2:4, :].rearrange("p a n -> p (a n)"), ACT.Identity, bias=b_dq[:, 0:1]).then_inc(act, 1)
                eng.wait_ge(pe, T_MT)
                for k in range(KD):
                    i = eng.activation(mergedT[:, :, k, :], p_b[:, 2 + k, 0:P].rearrange("p (b e) -> p e b", b=B), ACT.Copy)
                i.then_inc(act, 1)
                for half in range(2):
                    eng.wait_ge(pe, (T_QT0, T_QT1)[half])
                    for eo in range(2):
                        for k4 in range(4):
                            k = 4 * half + k4
                            i = eng.activation(
                                qT[:, eo, :].rearrange("p (b k e) -> p k b e", b=B, k=K8)[:, k],
                                (p_a, p_b)[half][:, eo, k4 * P:(k4 + 1) * P].rearrange("p (b e) -> p b e", b=B), ACT.Copy)
                    i.then_inc(act, 1)
                eng.wait_ge(act, A_QT1)
                eng.activation(qp[:, 0, :, :], qT[:, :, :], ACT.Copy).then_inc(act, 1)
                eng.wait_ge(dve, V_R1)
                eng.activation(qp[:, 1, :, :], qrest[:, :, :], ACT.Copy).then_inc(act, 1)

            @block.tensor
            def _(eng):
                eng.wait_ge(consts, 16 * 8)
                eng.wait_ge(dve, V_ROWS)
                for half in range(2):
                    for k in range(KD):
                        for k4 in range(4):
                            i = eng.transpose((p_a, p_b)[half][:, k, k4 * P:(k4 + 1) * P],
                                              xg_n[:, 4 * half + k4, k * P:(k + 1) * P], ident[:, :])
                    i.then_inc(pe, 1)
                eng.wait_ge(act, A_XGT1)
                for half in range(2):
                    for k in range(KD):
                        i = eng.matmul(p_a[:, 2 + half, :], w_dq[:, k, :], xgT[:, k, half * TT:(half + 1) * TT],
                                       start=k == 0, stop=k == KD - 1)
                i.then_inc(pe, 1)
                eng.wait_ge(dve, V_MERGED)
                for k in range(KD):
                    i = eng.transpose(p_b[:, 2 + k, 0:P], merged[:, k * P:(k + 1) * P], ident[:, :])
                i.then_inc(pe, 1)
                eng.wait_ge(act, A_MT)
                for half in range(2):
                    if half:
                        eng.wait_ge(dve, V_QR0)
                    for k4 in range(4):
                        k = 4 * half + k4
                        eng.matmul(p_a[:, k4, 0:D], ctqT[:, k * P:(k + 1) * P], w_uq[:, :], start=True, stop=True)
                        i = eng.matmul(p_b[:, k4, 0:D], ctqT[:, k * P:(k + 1) * P], w_qr[:, :], start=True, stop=True)
                    i.then_inc(pe, 1)
                eng.wait_ge(dve, V_QSUM)
                for half in range(2):
                    for eo in range(2):
                        for k4 in range(4):
                            i = eng.transpose((p_a, p_b)[half][:, eo, k4 * P:(k4 + 1) * P],
                                              qs[:, 4 * half + k4, eo * P:(eo + 1) * P], ident[:, :])
                    i.then_inc(pe, 1)


def attention_stage(nc, ins, scr, keep):
    with ExitStack() as ctx:
        sb = lambda n, s, d=F32: ctx.enter_context(nc.sbuf_tensor("a_" + n, s, d))
        ps = lambda n, s, d=F32: ctx.enter_context(nc.psum_tensor("a_" + n, s, d))
        sem = lambda n: ctx.enter_context(nc.semaphore("a_" + n))
        two = range(2)
        R, RM = 96, 99
        G = B * HG
        NM = 4 * 2 * NC
        NX = 4 * 8
        QUADS = NE // 4
        LEAD = 1
        QB = QUADS // B
        ident, mergedT, accT = keep["ident"], keep["mergedT"], keep["accT"]

        identb = sb("identb", [P, P], BF16)
        kst = [sb(f"kst{p}", [RM, NC, 4, TT], BF16) for p in two]
        qst = [sb(f"qst{p}", [RM, 4, SB], BF16) for p in two]
        vg = [sb(f"vg{p}", [P, NC, 4, 4 * VW]) for p in two]
        mpart = [sb(f"mpart{p}", [P, 8, NC]) for p in two]
        nmax = [sb(f"nmax{p}", [P, 8]) for p in two]
        nrest = [sb(f"nrest{p}", [P, 8]) for p in two]
        nrest2 = [sb(f"nrest2{p}", [P, 8]) for p in two]
        nparts = [sb(f"nparts{p}", [P, 3, 8], BF16) for p in two]
        nT = [sb(f"nT{p}", [24, P], BF16) for p in two]
        pr = [sb(f"pr{p}", [P, 4, 2, SB]) for p in two]
        w1 = sb("w1", [P, 4, KD, HID])
        w2 = sb("w2", [P, 4, 8, D])
        b1 = sb("b1", [P, NE, 8])
        mq = sb("mq", [P, 4, KD, B])
        hraw = sb("hraw", [P, HID])
        hT = sb("hT", [P, 8, 4, B])
        gl = sb("gl", [P, 8, 4, B])
        eo = sb("eo", [P, D])

        p_m = [ps(f"p_m{i}", [P, TT]) for i in range(4)]
        p_s = [ps(f"p_s{i}", [P, 2, SB]) for i in two]
        p_acc = ps("p_acc", [P, TT])
        p_e = ps("p_e", [P, TT])
        p_tr = p_e[:, :].bitcast(BF16)

        setup, ones_ok, consts = sem("setup"), sem("ones_ok"), sem("consts")
        g_in = [sem(f"g_in{p}") for p in two]
        nmax_in = [sem(f"nmax_in{p}") for p in two]
        sc_ok, red_ok, np_ok, tr_ok, nT_ok = (sem(n) for n in ("sc_ok", "red_ok", "np_ok", "tr_ok", "nT_ok"))
        neg_ok, hi_ok, r1_ok, mid_ok, r2_ok = (sem(n) for n in ("neg_ok", "hi_ok", "r1_ok", "mid_ok", "r2_ok"))
        s_ok, ex_ok, pv_ok, acc_ok, acc_out = (sem(n) for n in ("s_ok", "ex_ok", "pv_ok", "acc_ok", "acc_out"))
        w1_in, w2_in = sem("w1_in"), sem("w2_in")
        mq_ok, h_ok, hraw_ok, hTp_ok, hT_ok, hg_ok, o_ok, eo_ok, eo_out = (
            sem(n) for n in ("mq_ok", "h_ok", "hraw_ok", "hTp_ok", "hT_ok", "hg_ok", "o_ok", "eo_ok", "eo_out"))

        def passes(eng, step, tail=None):
            for hg in range(HG):
                step(hg, 0, hg)
            with eng.Fori(1, B) as b:
                for hg in range(HG):
                    step(b * HG + hg, b, hg)
            if tail:
                tail()

        def prev(g, b, hg):
            return (g - 1, b if hg else b - 1, (hg - 1) % HG)

        with nc.Block() as block:
            @block.sync
            def _(eng):
                eng.dma_start(b1[:, :, :], ins["b1T"]).then_inc(consts, 16)
                eng.wait_ge(ones_ok, 1)

                def load(g, b, hg):
                    p = hg % 2
                    wait(eng, pv_ok, 8 * (g - 1))
                    kp = scr["kp"].rearrange("(b c a r) n -> b a r c n", b=B, c=NC, a=HG)
                    for lo, n, src in ((0, 48, 0), (48, 32, 0), (80, 16, 0)):
                        eng.dma_start(kst[p][lo:lo + n, :, :, :].rearrange("r c z t -> r c (z t)"),
                                      kp[bass.ds(b, 1), hg, src:src + n, :, :].rearrange("o r c n -> (o r) c n")).then_inc(g_in[p], 16)
                    for g6, part in enumerate((0, 0, 0, 1, 1, 2)):
                        eng.dma_start(qst[p][g6 * 16:(g6 + 1) * 16, :, :].rearrange("r z t -> r (z t)"),
                                      scr["qp"][bass.ds(b, 1), hg, part * 64:(part + 1) * 64, :]
                                      .rearrange("o (r z) t -> (o r) (z t)", z=4)).then_inc(g_in[p], 16)
                    eng.dma_start(vg[p][:, :, :, :].rearrange("p c a v -> p c (a v)"), 
                                  scr["vp"].rearrange("(b c a) p n -> b a p c n", b=B, c=NC)[bass.ds(b, 1), hg]
                                  .rearrange("o p c n -> (o p) c n")).then_inc(g_in[p], 16)

                passes(eng, load)

            @block.gpsimd
            def _(eng):
                for p in two:
                    i = eng.memset(kst[p][R:RM, :, :, :], 1.0)
                i.then_inc(ones_ok, 1)

                def quad(g, b, hg):
                    if hg % 2 == 0:
                        return
                    q = b * QB + hg // 2
                    wait(eng, h_ok, q)
                    for j in range(4):
                        eng.dma_start(w1[:, j, :, :], ins["w1"][bass.ds(q * 4 + j, 1), 0:D, :]
                                      .rearrange("a (k p) n -> p (a k) n", p=P)).then_inc(w1_in, 16)
                    wait(eng, o_ok, q)
                    for j in range(4):
                        eng.dma_start(w2[:, j, :, :], ins["w2"][bass.ds(q * 4 + j, 1), 0:HID, :]
                                      .rearrange("a (k p) n -> p (a k) n", p=P)).then_inc(w2_in, 16)

                passes(eng, quad)

            @block.vector
            def _(eng):
                eng.memset(p_acc[:, :], 0.0)
                eng.memset(p_e[:, :], 0.0).then_inc(setup, 1)
                eng.tensor_copy(identb[:, :], ident[:, :]).then_inc(setup, 1)
                eng.wait_ge(consts, 16)

                def maxima(g, b, hg):
                    p = hg % 2
                    for i in range(NM):
                        eng.wait_ge(sc_ok, g * NM + i + 1)
                        if i == 0:
                            wait(eng, neg_ok, g - 1)
                        eng.tensor_reduce(mpart[p][:, i // NC, i % NC:i % NC + 1], p_m[i % 4][:, :], AX.X, ALU.max)\
                           .then_inc(red_ok, 1)
                    eng.wait_ge(red_ok, g * NM + NM)
                    eng.tensor_reduce(nmax[p][:, :], mpart[p][:, :, :], AX.X, ALU.max, negate=True).then_inc(neg_ok, 1)
                    eng.wait_ge(neg_ok, g + 1)
                    wait(eng, tr_ok, g - 1)
                    eng.tensor_copy(nparts[p][:, 0, :], nmax[p][:, :]).then_inc(hi_ok, 1)
                    eng.wait_ge(hi_ok, g + 1)
                    eng.tensor_tensor(nrest[p][:, :], nmax[p][:, :], nparts[p][:, 0, :], ALU.subtract).then_inc(r1_ok, 1)
                    eng.wait_ge(r1_ok, g + 1)
                    eng.tensor_copy(nparts[p][:, 1, :], nrest[p][:, :]).then_inc(mid_ok, 1)
                    eng.wait_ge(mid_ok, g + 1)
                    eng.tensor_tensor(nparts[p][:, 2, :], nrest[p][:, :], nparts[p][:, 1, :], ALU.subtract).then_inc(np_ok, 1)

                def take(g, b, hg):
                    eng.wait_ge(pv_ok, g * 8 + 8)
                    eng.tensor_copy(accT[:, hg, :, bass.ds(b, 1), :].rearrange("p k o e -> p k (o e)"),
                                    p_acc[:, 0:SB].rearrange("p (k e) -> p k e", k=TOPK)).then_inc(acc_out, 1)

                def step(g, b, hg):
                    maxima(g, b, hg)
                    if hg % 2:
                        q = b * QB + hg // 2
                        wait(eng, h_ok, q)
                        eng.tensor_copy(mq[:, :, :, :].rearrange("p j k b -> p (j k b)"),
                                        mergedT[:, bass.ds(q * 4, 4), :, :].rearrange("p j k b -> p (j k b)")).then_inc(mq_ok, 1)
                    if not (isinstance(g, int) and g == 0):
                        take(*prev(g, b, hg))
                    if hg % 2:
                        eng.wait_ge(hTp_ok, q + 1)
                        wait(eng, hg_ok, q)
                        for k in two:
                            i = eng.tensor_tensor(hT[:, 4 * k:4 * k + 4, :, :],
                                                  p_m[2 + k][:, :].rearrange("p (c j e) -> p c j e", c=4, j=4)[:, :, :, 0:B],
                                                  b1[:, bass.ds(q * 4, 4), 4 * k:4 * k + 4].rearrange("p j c -> p c j")
                                                  .unsqueeze(3).broadcast_to([P, 4, 4, B]), ALU.add)
                        i.then_inc(hT_ok, 1)

                passes(eng, step, lambda: take(G - 1, B - 1, HG - 1))

            @block.scalar
            def _(eng):
                def negT(g, b, hg):
                    p = hg % 2
                    eng.wait_ge(tr_ok, g + 1)
                    wait(eng, nmax_in[p], b * 32 + (hg // 2) * 16)
                    eng.activation(nT[p][:, :], p_tr[0:24, 0:P], ACT.Copy).then_inc(nT_ok, 1)
                    eng.wait_ge(nT_ok, g + 1)
                    eng.dma_start(qst[p][R:RM, :, :].rearrange("r z (m t) -> r (z m) t", m=2), nT[p][:, :]).then_inc(nmax_in[p], 16)

                def exps(g, b, hg):
                    for c in range(8):
                        for hh in range(4):
                            n = 4 * c + hh
                            eng.wait_ge(s_ok, g * NX + n + 1)
                            if hh == 0:
                                wait(eng, pv_ok, g * 8 + c - 1)
                            eng.activation(pr[c % 2][:, hh, :, :], p_s[n % 2][:, :, :], ACT.Exp, scale=ATT).then_inc(ex_ok, 1)

                def step(g, b, hg):
                    if not (isinstance(g, int) and g == 0):
                        exps(*prev(g, b, hg))
                    negT(g, b, hg)
                    if hg % 2:
                        q = b * QB + hg // 2
                        eng.wait_ge(h_ok, q + 1)
                        for k in two:
                            i = eng.activation(hraw[:, k * TT:(k + 1) * TT], p_m[k][:, :], ACT.Copy)
                        i.then_inc(hraw_ok, 1)
                        eng.wait_ge(hT_ok, q + 1)
                        eng.activation(hg_t, hT[:, :, :, :], ACT.Gelu).then_inc(hg_ok, 1)
                        eng.wait_ge(o_ok, q + 1)
                        wait(eng, eo_out, q * 64)
                        eng.activation(eo[:, :], p_e[:, 0:D], ACT.Copy).then_inc(eo_ok, 1)
                        eng.wait_ge(eo_ok, q + 1)
                        for j in range(4):
                            eng.dma_start(scr["oe"][:, bass.ds(q * 4 + j, 1), :].rearrange("b a n -> b (a n)"),
                                          eo[32 * j:32 * j + B, :]).then_inc(eo_out, 16)

                hg_t = gl[:, :, :, :]
                passes(eng, step, lambda: exps(G - 1, B - 1, HG - 1))
                eng.wait_ge(eo_out, 64 * QUADS)

            @block.tensor
            def _(eng):
                eng.wait_ge(setup, 2)
                eng.wait_ge(ones_ok, 1)

                def scores(g, b, hg, tiles):
                    p = hg % 2
                    for i in tiles:
                        if i == 0:
                            eng.wait_ge(g_in[p], b * 320 + (hg // 2) * 160 + 160)
                        hh, m, c = i // 8, (i // 4) % 2, i % 4
                        if i < 4:
                            wait(eng, red_ok, g * NM)
                            if hg % 2 == 0:
                                wait(eng, hT_ok, b * QB + hg // 2)
                        else:
                            eng.wait_ge(red_ok, g * NM + i - 3)
                        eng.matmul(p_m[i % 4][:, :], qst[p][0:R, hh, m * P:(m + 1) * P], kst[p][0:R, c, hh, :],
                                   start=True, stop=True).then_inc(sc_ok, 1)

                def transpose_max(g, b, hg):
                    eng.wait_ge(np_ok, g + 1)
                    if hg % 2 == 0:
                        wait(eng, eo_ok, b * QB + hg // 2)
                    wait(eng, nT_ok, g)
                    eng.transpose(p_tr[0:24, 0:P], nparts[hg % 2][:, :, :].rearrange("p a b -> p (a b)"), identb[:, :])\
                       .then_inc(tr_ok, 1)

                def weigh(g, b, hg, following=None):
                    p = hg % 2
                    eng.wait_ge(nmax_in[p], b * 32 + (hg // 2) * 16 + 16)

                    def values(c):
                        eng.wait_ge(ex_ok, g * NX + 4 * c + 4)
                        if c == 0:
                            wait(eng, acc_out, g)
                        for k2 in range(2):
                            kt = 2 * c + k2
                            for hh in range(4):
                                i = eng.matmul(p_acc[32 * hh:32 * hh + VW, 0:SB], vg[p][:, kt // 4, kt % 4, hh * VW:(hh + 1) * VW],
                                               pr[c % 2][:, hh, k2, :], start=kt == 0, stop=kt == 15)
                        i.then_inc(pv_ok, 1)

                    for c in range(8):
                        for hh in range(4):
                            n = 4 * c + hh
                            wait(eng, ex_ok, g * NX + n - 1)
                            for k2 in range(2):
                                kt = 2 * c + k2
                                i = eng.matmul(p_s[n % 2][:, k2, :], kst[p][0:RM, kt // 4, hh, (kt % 4) * P:(kt % 4 + 1) * P],
                                               qst[p][0:RM, hh, :], start=True, stop=True)
                            i.then_inc(s_ok, 1)
                            if following and c >= LEAD:
                                j, slots = (c - LEAD) * 4 + hh, (8 - LEAD) * 4
                                scores(*following, range(NM * j // slots, NM * (j + 1) // slots))
                        if c:
                            values(c - 1)
                    values(7)

                def quad(b, hg):
                    q = b * QB + hg // 2
                    eng.wait_ge(mq_ok, q + 1)
                    eng.wait_ge(w1_in, q * 64 + 64)
                    eng.wait_ge(red_ok, (b * HG + hg + 1) * NM)
                    for half in two:
                        for k in range(KD):
                            for j in range(4):
                                i = eng.matmul(p_m[half][32 * j:32 * j + B, :], mq[:, j, k, :], w1[:, j, k, half * TT:(half + 1) * TT],
                                               start=k == 0, stop=k == KD - 1)
                    i.then_inc(h_ok, 1)
                    eng.wait_ge(hraw_ok, q + 1)
                    for c in range(8):
                        i = eng.transpose(p_m[2 + c // 4][:, (c % 4) * P:(c % 4 + 1) * P], hraw[:, c * P:(c + 1) * P], ident[:, :])
                    i.then_inc(hTp_ok, 1)
                    eng.wait_ge(w2_in, q * 64 + 64)
                    eng.wait_ge(hg_ok, q + 1)
                    for c in range(8):
                        for j in range(4):
                            i = eng.matmul(p_e[32 * j:32 * j + B, 0:D], gl[:, c, j, :], w2[:, j, c, :], start=c == 0, stop=c == 7)
                    i.then_inc(o_ok, 1)

                def step(g, b, hg):
                    if isinstance(g, int) and g == 0:
                        scores(g, b, hg, range(NM))
                    else:
                        weigh(*prev(g, b, hg), following=(g, b, hg))
                    transpose_max(g, b, hg)
                    if hg % 2:
                        quad(b, hg)

                passes(eng, step, lambda: weigh(G - 1, B - 1, HG - 1))


def scatter_stage(nc, ins, scr, keep):
    with ExitStack() as ctx:
        sb = lambda n, s, d=F32: ctx.enter_context(nc.sbuf_tensor("c_" + n, s, d))
        ps = lambda n, s, d=F32: ctx.enter_context(nc.psum_tensor("c_" + n, s, d))
        sem = lambda n: ctx.enter_context(nc.semaphore("c_" + n))
        two = range(2)
        K8 = TOPK
        ident, xg, vals, gf, accT = (keep[n] for n in ("ident", "xg", "vals", "gf", "accT"))
        w_o = sb("w_o", [P, KD, D])
        b_o = sb("b_o", [P, D])
        b2 = sb("b2", [P, D])
        oe = sb("oe", [P, D])
        oeb = sb("oeb", [P, D])
        rowb = sb("rowb", [P, NS])
        rankb = sb("rankb", [P, NS])
        rank = sb("rank", [P, K8])
        share = sb("share", [P, NS])
        part = [sb(f"part{k}", [P, NS]) for k in two]
        seen = [sb(f"seen{k}", [P, NS]) for k in two]
        top = sb("top", [P, K8])
        dup = sb("dup", [P, K8])
        target = sb("target", [P, K8], U32)
        rec = [sb(f"rec{p}", [P, NH]) for p in two]
        on = [sb(f"on{p}", [P, NH, HD]) for p in two]
        oT = [sb(f"oT{p}", [P, KD, P]) for p in two]
        sg = [sb(f"sg{p}", [P, D]) for p in two]
        s0 = [sb(f"s0{p}", [P, D]) for p in two]
        s1 = [sb(f"s1{p}", [P, D]) for p in two]
        xo = sb("xo", [P, K8, D])
        p_o = [ps(f"p_o{p}", [P, NH, 32]) for p in two]
        p_t = [ps(f"p_t{p}", [P, KD, P]) for p in two]
        p_x = [ps(f"p_x{p}", [P, 2, D]) for p in two]
        c_in = sem("c_in")
        share_ok, part_ok, seen_ok, top_ok, dup_ok, target_ok, oeb_ok = (
            sem(n) for n in ("share_ok", "part_ok", "seen_ok", "top_ok", "dup_ok", "target_ok", "oeb_ok"))
        po_ok, rec_ok, on_ok, pt_ok, oT_ok, px_ok, sg_ok, s0_ok, s1_ok, xo_ok, out_ok = (
            sem(n) for n in ("po_ok", "rec_ok", "on_ok", "pt_ok", "oT_ok", "px_ok", "sg_ok", "s0_ok", "s1_ok", "xo_ok", "out_ok"))
        N_IN = 7 + B

        with nc.Block() as block:
            @block.sync
            def _(eng):
                rows = scr["rows"].rearrange("p k -> (p k)")
                for dst, src in ((rowb[:, :], rows.partition_broadcast(P)),
                                 (rankb[:, :], ins["rank"].rearrange("p k -> (p k)").partition_broadcast(P)),
                                 (rank[:, :], ins["rank"]),
                                 (oe[:, :], scr["oe"].rearrange("b e n -> (b e) n")),
                                 (w_o[:, :, :], ins["Wo"].rearrange("(k p) m -> p k m", p=P)),
                                 (b_o[:, :], ins["b_o"].partition_broadcast(P))):
                    eng.dma_start(dst, src).then_inc(c_in, 16)
                for b in range(B):
                    eng.dma_start(b2[b * NE:(b + 1) * NE, :], ins["b2"]).then_inc(c_in, 16)
                eng.dma_start(dup[:, :], ins["rank"]).then_inc(c_in, 16)

            @block.vector
            def _(eng):
                eng.wait_ge(c_in, 16 * N_IN)
                eng.tensor_tensor(oeb[:, :], oe[:, :], b2[:, :], ALU.add).then_inc(oeb_ok, 1)
                eng.tensor_scalar(share[:, :], rowb[:, :], gf[:, 0:1], vals[:, 0:1], ALU.is_equal, ALU.mult).then_inc(share_ok, 1)
                for k in range(1, K8):
                    wait(eng, share_ok, k - 1)
                    eng.tensor_scalar(part[k % 2][:, :], rowb[:, :], gf[:, k:k + 1], vals[:, k:k + 1], ALU.is_equal, ALU.mult)\
                       .then_inc(part_ok, 1)
                    eng.wait_ge(part_ok, k)
                    eng.wait_ge(share_ok, k)
                    eng.tensor_tensor(share[:, :], share[:, :], part[k % 2][:, :], ALU.add).then_inc(share_ok, 1)
                for k in range(K8):
                    wait(eng, top_ok, k - 1)
                    eng.scalar_tensor_tensor(seen[k % 2][:, :], rowb[:, :], gf[:, k:k + 1], rankb[:, :], ALU.is_equal, ALU.mult)\
                       .then_inc(seen_ok, 1)
                    eng.wait_ge(seen_ok, k + 1)
                    eng.tensor_reduce(top[:, k:k + 1], seen[k % 2][:, :], AX.X, ALU.max).then_inc(top_ok, 1)
                eng.wait_ge(top_ok, K8)
                eng.tensor_tensor(dup[:, :], top[:, :], rank[:, :], ALU.is_gt).then_inc(dup_ok, 1)
                eng.wait_ge(dup_ok, 1)
                eng.scalar_tensor_tensor(target[:, :], dup[:, :], float(8 * B * S), gf[:, :], ALU.mult, ALU.add).then_inc(target_ok, 1)

                def heads(k):
                    p = k % 2
                    eng.wait_ge(po_ok, k + 1)
                    eng.reciprocal(rec[p][:, :], p_o[p][:, :, HD]).then_inc(rec_ok, 1)
                    eng.wait_ge(rec_ok, k + 1)
                    wait(eng, pt_ok, k - 1)
                    eng.tensor_tensor(on[p][:, :, :], p_o[p][:, :, 0:HD], rec[p][:, :].unsqueeze(2).broadcast_to([P, NH, HD]),
                                      ALU.mult).then_inc(on_ok, 1)

                def rows(k):
                    p = k % 2
                    eng.wait_ge(px_ok, k + 1)
                    wait(eng, s1_ok, k - 1)
                    eng.tensor_tensor(s0[p][:, :], p_x[p][:, 0, :], b_o[:, :], ALU.add).then_inc(s0_ok, 1)
                    eng.wait_ge(s0_ok, k + 1)
                    eng.wait_ge(sg_ok, k + 1)
                    wait(eng, xo_ok, k - 1)
                    eng.tensor_tensor(s1[p][:, :], s0[p][:, :], sg[p][:, :], ALU.mult).then_inc(s1_ok, 1)
                    eng.wait_ge(s1_ok, k + 1)
                    eng.tensor_tensor(xo[:, k, :], s1[p][:, :], xg[:, k, :], ALU.add).then_inc(xo_ok, 1)

                for k in range(K8 + 1):
                    if k < K8:
                        heads(k)
                    if k:
                        rows(k - 1)

            @block.scalar
            def _(eng):
                for k in range(K8):
                    p = k % 2
                    eng.wait_ge(pt_ok, k + 1)
                    eng.activation(oT[p][:, :, :], p_t[p][:, :, :], ACT.Copy).then_inc(oT_ok, 1)
                    eng.wait_ge(s0_ok, k + 1)
                    wait(eng, s1_ok, k - 1)
                    eng.activation(sg[p][:, :], p_x[p][:, 1, :], ACT.Silu).then_inc(sg_ok, 1)

            @block.tensor
            def _(eng):
                eng.wait_ge(c_in, 16 * N_IN)

                def turn(k):
                    p = k % 2
                    wait(eng, on_ok, k - 1)
                    for hg in range(HG):
                        i = eng.transpose(p_o[p][:, :, :].rearrange("p h w -> p (h w)")[:, hg * P:(hg + 1) * P],
                                          accT[:, hg, k, :, :].rearrange("p b e -> p (b e)"), ident[:, :])
                    i.then_inc(po_ok, 1)

                turn(0)
                for k in range(K8):
                    p = k % 2
                    if k + 1 < K8:
                        turn(k + 1)
                    eng.wait_ge(on_ok, k + 1)
                    wait(eng, oT_ok, k - 1)
                    for d in range(KD):
                        i = eng.transpose(p_t[p][:, d, :], on[p][:, :, :].rearrange("p h w -> p (h w)")[:, d * P:(d + 1) * P], ident[:, :])
                    i.then_inc(pt_ok, 1)
                    eng.wait_ge(oT_ok, k + 1)
                    wait(eng, s0_ok, k - 1)
                    wait(eng, sg_ok, k - 1)
                    for d in range(KD):
                        eng.matmul(p_x[p][:, 0, :], oT[p][:, d, :], w_o[:, d, :], start=d == 0, stop=d == KD - 1)
                    if k == 0:
                        eng.wait_ge(share_ok, K8)
                        eng.wait_ge(oeb_ok, 1)
                    eng.matmul(p_x[p][:, 1, :], share[:, :].rearrange("p (s k) -> p k s", k=K8)[:, k, :], oeb[:, :],
                               start=True, stop=True).then_inc(px_ok, 1)

            @block.gpsimd
            def _(eng):
                eng.wait_ge(target_ok, 1)
                for k in range(K8):
                    eng.wait_ge(xo_ok, k + 1)
                    eng.indirect_dma_start(scr["x1"], bass.IndirectOffsetOnAxis(target[:, k:k + 1], 0), xo[:, k, :], None,
                                           bounds_check=B * S - 1, oob_is_err=False).then_inc(out_ok, 16)
                eng.wait_ge(out_ok, 16 * K8)


def layer1_stage(nc, ins, scr):
    with ExitStack() as ctx:
        sb = lambda n, s, d=F32: ctx.enter_context(nc.sbuf_tensor("l_" + n, s, d))
        ps = lambda n, s, d=F32: ctx.enter_context(nc.psum_tensor("l_" + n, s, d))
        sem = lambda n: ctx.enter_context(nc.semaphore("l_" + n))
        two = range(2)
        NX = 3 * 2 * NST + RK
        RINGS = 4

        ident = sb("ident", [P, P])
        w_in = sb("w_in", [P, KD, 2 * DI])
        b_in = sb("b_in", [P, 2 * CB])
        w_out = sb("w_out", [P, CB, D])
        w_x = sb("w_x", [P, CB, NX])
        w_dt = sb("w_dt", [NX, DI])
        w_g = sb("w_g", [P, KD, FH])
        w_u = sb("w_u", [P, KD, FH])
        w_d = sb("w_d", [P, FB, D])
        a_neg = sb("a_neg", [P, CB, NST])
        conv_w = sb("conv_w", [P, CB, 4])
        conv_b = sb("conv_b", [P, CB])
        skip = sb("skip", [P, CB])
        dt_b = sb("dt_b", [P, CB])
        b_out = sb("b_out", [P, D])
        mask = sb("mask", [P, NT + 1])
        pick = sb("pick", [3 * 2 * NST, 2 * NST], BF16)
        eps = sb("eps", [P, 1])
        spare = sb("spare", [P, 1])
        hl = sb("hl", [P, NST, CB])

        p_w = [ps(f"p_w{i}", [P, TT]) for i in two]
        p_b, p_c = ps("p_b", [P, TT]), ps("p_c", [P, TT])
        p_y = ps("p_y", [P, CB, TT])
        loaded, cast, made, a_ok, copied = sem("loaded"), sem("cast"), sem("made"), sem("a_ok"), sem("copied")

        with ExitStack() as inner:
            ib = lambda n, s, d=F32: inner.enter_context(nc.sbuf_tensor("lw_" + n, s, d))
            fc1 = ib("fc1", [P, KD, D])
            fc1_b = ib("fc1_b", [P, KD])
            in_t = ib("in_t", [P, KD, 2 * DI])
            outp = ib("outp", [P, KD, DI])
            fc2_t = ib("fc2_t", [P, KD, D])
            g_int, u_int = ib("g_int", [P, KD, FH], I32), ib("u_int", [P, KD, FH], I32)
            d_int = ib("d_int", [P, FB, D], I32)
            pick32 = ib("pick32", [3 * 2 * NST, 2 * NST])
            a_exp = ib("a_exp", [P, CB, NST])
            N_LOAD = 20
            with nc.Block() as block:
                @block.sync
                def _(eng):
                    for dst, src in ((ident[:, :], ins["ident"]),
                                     (fc1[:, :, :], ins["fc1_w"].rearrange("(k p) i -> p k i", p=P)),
                                     (fc1_b[:, :], ins["fc1_b"]),
                                     (in_t[:, :, :], ins["in_projT"].rearrange("(k p) o -> p k o", p=P)),
                                     (outp[:, :, :], ins["out_proj_w"].rearrange("(k p) c -> p k c", p=P)),
                                     (fc2_t[:, :, :], ins["fc2_wT"].rearrange("(k p) o -> p k o", p=P)),
                                     (g_int[:, :, :], ins["wgT"].rearrange("(k p) h -> p k h", p=P)),
                                     (u_int[:, :, :], ins["wuT"].rearrange("(k p) h -> p k h", p=P)),
                                     (d_int[:, :, :], ins["wdT"].rearrange("(k p) o -> p k o", p=P)),
                                     (pick32[:, :], ins["pick"]),
                                     (a_exp[:, :, :], ins["A_log"].rearrange("(k p) n -> p k n", p=P)),
                                     (w_x[:, :, :], ins["x_projT"].rearrange("(k p) n -> p k n", p=P)),
                                     (w_dt[NX - RK:NX, :], ins["dt_projT"]),
                                     (conv_w[:, :, :], ins["conv_w"].rearrange("(k p) n -> p k n", p=P)),
                                     (conv_b[:, :], ins["conv_b"]), (skip[:, :], ins["skip"]), (dt_b[:, :], ins["dt_b"]),
                                     (b_out[:, :], ins["fc2_b"].partition_broadcast(P)),
                                     (mask[:, :], ins["mask"])):
                        eng.dma_start(dst, src).then_inc(loaded, 16)
                    eng.wait_ge(loaded, 16 * (N_LOAD - 1))

                @block.vector
                def _(eng):
                    eng.wait_ge(loaded, 16 * (N_LOAD - 1))
                    eng.tensor_copy(pick[:, :], pick32[:, :])
                    eng.tensor_copy(w_g[:, :, :], g_int[:, :, :])
                    eng.tensor_copy(w_u[:, :, :], u_int[:, :, :])
                    eng.tensor_copy(w_d[:, :, :], d_int[:, :, :])
                    eng.memset(eps[:, :], EPS)
                    eng.memset(hl[:, :, :], 0.0).then_inc(cast, 1)
                    eng.wait_ge(a_ok, 1)
                    eng.tensor_scalar(a_neg[:, :, :], a_exp[:, :, :], -1.0, None, ALU.mult)

                @block.scalar
                def _(eng):
                    eng.wait_ge(loaded, 16 * (N_LOAD - 1))
                    eng.activation(a_exp[:, :, :], a_exp[:, :, :], ACT.Exp).then_inc(a_ok, 1)
                    for i in range(4):
                        eng.wait_ge(made, i + 1)
                        eng.activation(w_in[:, i // 2, (i % 2) * TT:(i % 2 + 1) * TT], p_w[i % 2][:, :], ACT.Copy).then_inc(copied, 1)
                    eng.wait_ge(made, 5)
                    eng.activation(b_in[:, :], p_b[:, 0:2 * CB], ACT.Copy)
                    for c in range(CB):
                        i = eng.activation(w_out[:, c, :], p_y[:, c, 0:D], ACT.Copy)

                @block.tensor
                def _(eng):
                    eng.wait_ge(loaded, 16 * (N_LOAD - 1))
                    for i in range(4):
                        wait(eng, copied, i - 1)
                        for k in range(KD):
                            m = eng.matmul(p_w[i % 2][:, :], fc1[:, k, (i // 2) * P:(i // 2 + 1) * P],
                                           in_t[:, k, (i % 2) * TT:(i % 2 + 1) * TT], start=k == 0, stop=k == KD - 1)
                        m.then_inc(made, 1)
                    for o in range(2 * CB):
                        for k in range(KD):
                            eng.matmul(p_b[:, o:o + 1], in_t[:, k, o * P:(o + 1) * P], fc1_b[:, k:k + 1],
                                       start=k == 0, stop=k == KD - 1)
                    for c in range(CB):
                        for k in range(KD):
                            m = eng.matmul(p_y[:, c, 0:D], outp[:, k, c * P:(c + 1) * P], fc2_t[:, k, :],
                                           start=k == 0, stop=k == KD - 1)
                    m.then_inc(made, 1)

        x_new = sb("x_new", [P, 4, D])
        x_old = sb("x_old", [P, 4, D])
        res = sb("res", [P, 4, D])
        stats = sb("stats", [P, 4, 6])
        mv = sb("mv", [P, 4, 2])
        std = sb("std", [P, 4])
        rstd = sb("rstd", [P, 4])
        xn = sb("xn", [P, 4, D])
        xnT = [sb(f"xnT{p}", [P, KD, TT]) for p in two]
        xc = sb("xc", [P, CB, TT + 3])
        u = [sb(f"u{p}", [P, CB, TT]) for p in two]
        dt = [sb(f"dt{p}", [P, CB, TT]) for p in two]
        dtu = [sb(f"dtu{p}", [P, CB, TT]) for p in two]
        sz = sb("sz", [P, CB, TT])
        bc = sb("bc", [3 * 2 * NST, TT])
        stk = [sb(f"stk{p}", [3 * 2 * NST, TT], BF16) for p in two]
        mid = sb("mid", [3 * 2 * NST, TT], BF16)
        low = sb("low", [NX, TT])
        sg = sb("sg", [P, TT])
        hT = sb("hT", [P, FB, TT])
        gate = sb("gate", [P, 4, D])
        bs = [sb(f"bs{p}", [P, TT]) for p in two]
        dA = [sb(f"dA{p}", [P, CB, TT]) for p in two]
        st = [sb(f"st{r}", [P, CB, TT]) for r in range(RINGS)]

        x_in, old_in, out_st = sem("x_in"), sem("old_in"), sem("out_st")
        stats_ok, aggr_ok, std_ok, rstd_ok, xn_ok, tr_ok, xnT_ok = (
            sem(n) for n in ("stats_ok", "aggr_ok", "std_ok", "rstd_ok", "xn_ok", "tr_ok", "xnT_ok"))
        xc_pe, xc_ok, z_pe, z_ok, conv_ok, carry_ok, u_ok = (
            sem(n) for n in ("xc_pe", "xc_ok", "z_pe", "z_ok", "conv_ok", "carry_ok", "u_ok"))
        xd_pe, xd_ok, hi_ok, r1_ok, mid_ok, stk_ok = (sem(n) for n in ("xd_pe", "xd_ok", "hi_ok", "r1_ok", "mid_ok", "stk_ok"))
        dt_pe, abs_ok, exp_ok, ln_ok, dt_ok, dtu_ok = (sem(n) for n in ("dt_pe", "abs_ok", "exp_ok", "ln_ok", "dt_ok", "dtu_ok"))
        gu_pe, sg_ok, h_ok, dn_pe, g_ok = (sem(n) for n in ("gu_pe", "sg_ok", "h_ok", "dn_pe", "g_ok"))
        b_pe, bs_ok, c_pe, dA_ok, dbu_ok, scan_ok, hl_ok, prod_ok, y_pe = (
            sem(n) for n in ("b_pe", "bs_ok", "c_pe", "dA_ok", "dbu_ok", "scan_ok", "hl_ok", "prod_ok", "y_pe"))
        yd_ok, yg_ok, op_pe, t_ok, tg_ok, res_ok = (sem(n) for n in ("yd_ok", "yg_ok", "op_pe", "t_ok", "tg_ok", "res_ok"))

        DN, OUT, TR, XC0, XC1, Z0, Z1, GU0, XD, GU1, DT0, DT1, GU2, GU3, GU4, GU5 = range(NST)
        GU = (GU0, GU1, GU2, GU3, GU4, GU5)

        def periods(eng, period):
            period(0, 0, True, False, False)
            period(1, 1, True, True, False)
            with eng.Fori(0, (NT - 2) // 2) as j:
                for p in two:
                    period(j * 2 + (2 + p), p, True, True, True)
            period(NT, 0, False, True, True)
            period(NT + 1, 1, False, False, True)

        def rows(dram, t):
            return dram[bass.ds(t * TT, TT), :].rearrange("(a p) d -> p a d", p=P)

        with nc.Block() as block:
            @block.sync
            def _(eng):
                def period(q, p, front, scan, end):
                    if front:
                        wait(eng, xn_ok, q)
                        eng.dma_start(x_new[:, :, :], rows(scr["x1"], q)).then_inc(x_in, 16)
                    if end:
                        eng.wait_ge(old_in, (q - 2) * 16 + 16)
                        eng.wait_ge(res_ok, q - 1)
                        eng.dma_start(rows(scr["out"], q - 2), res[:, :, :]).then_inc(out_st, 16)
                    if scan:
                        wait(eng, res_ok, q - 1)
                        eng.dma_start(x_old[:, :, :], rows(scr["x1"], q - 1)).then_inc(old_in, 16)

                periods(eng, period)
                eng.wait_ge(out_st, 16 * NT)

            @block.vector
            def _(eng):
                eng.memset(xc[:, :, 0:3], 0.0).then_inc(carry_ok, 1)

                def scans(s, ps_, n):
                    g = s * NST + n
                    eng.wait_ge(dbu_ok, g + 1)
                    eng.wait_ge(dA_ok, g + 1)
                    wait(eng, hl_ok, g - NST + 1)
                    for c in range(CB):
                        i = eng.tensor_tensor_scan(st[n % RINGS][:, c, :], dA[n % 2][:, c, :], st[n % RINGS][:, c, :],
                                                   hl[:, n, c:c + 1], ALU.mult, ALU.add)
                    i.then_inc(scan_ok, 1)

                def last(s, ps_, n):
                    g = s * NST + n
                    eng.wait_ge(scan_ok, g + 1)
                    eng.tensor_tensor(hl[:, n, :], st[n % RINGS][:, :, TT - 1], mask[:, bass.ds(s + 1, 1)].broadcast_to([P, CB]),
                                      ALU.mult).then_inc(hl_ok, 1)

                def products(s, ps_, n):
                    g = s * NST + n
                    eng.wait_ge(c_pe, g + 1)
                    eng.wait_ge(hl_ok, g + 1)
                    eng.tensor_tensor(st[n % RINGS][:, :, :], st[n % RINGS][:, :, :],
                                      p_c[:, :].unsqueeze(1).broadcast_to([P, CB, TT]), ALU.mult).then_inc(prod_ok, 1)

                def conv(q, p, half):
                    base = q * 8 + half * 4
                    eng.wait_ge(xc_ok, q * 2 + half + 1)
                    for w in range(4):
                        wait(eng, conv_ok, base + w)
                        for c in (2 * half, 2 * half + 1):
                            if w == 0:
                                i = eng.tensor_scalar(u[p][:, c, :], xc[:, c, 0:TT], conv_w[:, c, 0:1], conv_b[:, c:c + 1],
                                                      ALU.mult, ALU.add)
                            else:
                                i = eng.scalar_tensor_tensor(u[p][:, c, :], xc[:, c, w:w + TT], conv_w[:, c, w:w + 1],
                                                             u[p][:, c, :], ALU.mult, ALU.add)
                        i.then_inc(conv_ok, 1)

                def hidden(t, i):
                    eng.wait_ge(gu_pe, t * FB + i + 1)
                    eng.wait_ge(sg_ok, t * FB + i + 1)
                    if i == 0:
                        wait(eng, dn_pe, t)
                    eng.scalar_tensor_tensor(hT[:, i, :], p_w[1][:, :], 1.0 / 127.0, sg[:, :], ALU.mult, ALU.mult).then_inc(h_ok, 1)

                def period(q, p, front, scan, end):
                    s, f = q - 1, q - 2
                    ps_ = 1 - p
                    for n in range(NST):
                        if scan:
                            scans(s, ps_, n)
                        if end and n == 1:
                            eng.wait_ge(y_pe, f * NST + NST)
                            for c in range(CB):
                                i = eng.scalar_tensor_tensor(u[p][:, c, :], u[p][:, c, :], skip[:, c:c + 1], p_y[:, c, :],
                                                             ALU.mult, ALU.add)
                            i.then_inc(yd_ok, 1)
                        if n:
                            if scan:
                                products(s, ps_, n - 1)
                        elif end:
                            products(f, p, NST - 1)
                        if scan:
                            last(s, ps_, n)
                        if scan and n - 1 in GU:
                            hidden(s, GU.index(n - 1))
                        if end and n == 0:
                            hidden(f, FB - 1)
                        if end and n == 1:
                            eng.wait_ge(yd_ok, f + 1)
                            eng.wait_ge(z_ok, f * 2 + 2)
                            eng.tensor_tensor(u[p][:, :, :], u[p][:, :, :], sz[:, :, :], ALU.mult).then_inc(yg_ok, 1)
                        if end and n == OUT + 1:
                            eng.wait_ge(op_pe, f + 1)
                            wait(eng, out_st, f * 16)
                            for h in two:
                                i = eng.tensor_tensor(res[:, 2 * h:2 * h + 2, :], p_w[h][:, :].rearrange("p (a d) -> p a d", a=2),
                                                      b_out[:, :].unsqueeze(1).broadcast_to([P, 2, D]), ALU.add)
                            i.then_inc(t_ok, 1)
                        if front and n == TR - 2:
                            eng.wait_ge(x_in, q * 16 + 16)
                            for a in range(4):
                                i = eng.bn_stats(stats[:, a, :], x_new[:, a, :])
                            i.then_inc(stats_ok, 1)
                            eng.wait_ge(stats_ok, q + 1)
                            eng.memset(spare[:, :], 0.0)
                            for a in range(4):
                                i = eng.bn_aggr(mv[:, a, :], stats[:, a, :])
                            i.then_inc(aggr_ok, 1)
                        if front and n == TR - 1:
                            eng.wait_ge(std_ok, q + 1)
                            wait(eng, tr_ok, q)
                            eng.reciprocal(rstd[:, :], std[:, :]).then_inc(rstd_ok, 1)
                            eng.wait_ge(rstd_ok, q + 1)
                            for a in range(4):
                                i = eng.tensor_scalar(xn[:, a, :], x_new[:, a, :], mv[:, a, 0:1], rstd[:, a:a + 1],
                                                      ALU.subtract, ALU.mult)
                            i.then_inc(xn_ok, 1)
                        if front and n == XC0 + 1:
                            if end:
                                eng.wait_ge(op_pe, f + 1)
                            conv(q, p, 0)
                        if front and n == XC1 + 1:
                            conv(q, p, 1)
                            eng.wait_ge(conv_ok, q * 8 + 8)
                            eng.tensor_tensor(xc[:, :, 0:3], xc[:, :, TT:TT + 3],
                                              mask[:, bass.ds(q + 1, 1)].unsqueeze(2).broadcast_to([P, CB, 3]), ALU.mult)\
                               .then_inc(carry_ok, 1)
                        if front and n == XD + 1:
                            eng.wait_ge(hi_ok, q + 1)
                            eng.tensor_tensor(bc[:, :], bc[:, :], stk[p][:, :], ALU.subtract).then_inc(r1_ok, 1)
                        if front and n == XD + 3:
                            eng.wait_ge(mid_ok, q + 1)
                            eng.wait_ge(r1_ok, q + 1)
                            eng.tensor_copy(stk[p][2 * NST:4 * NST, :], mid[2 * NST:4 * NST, :])
                            eng.tensor_tensor(stk[p][4 * NST:6 * NST, :], bc[4 * NST:6 * NST, :], mid[4 * NST:6 * NST, :],
                                              ALU.subtract).then_inc(stk_ok, 1)
                periods(eng, period)

            @block.gpsimd
            def _(eng):
                def dbu(s, ps_, n):
                    g = s * NST + n
                    eng.wait_ge(bs_ok, g + 1)
                    wait(eng, y_pe, g - RINGS + 1)
                    eng.tensor_tensor(st[n % RINGS][:, :, :], dtu[ps_][:, :, :],
                                      bs[n % 2][:, :].unsqueeze(1).broadcast_to([P, CB, TT]), ALU.mult).then_inc(dbu_ok, 1)

                def step_size(q, p, half):
                    cc = slice(2 * half, 2 * half + 2)
                    eng.wait_ge(ln_ok, q * 2 + half + 1)
                    eng.tensor_tensor(dt[p][:, cc, :], dt[p][:, cc, :], dtu[p][:, cc, :], ALU.add).then_inc(dt_ok, 1)

                def step_input(q, p, half):
                    cc = slice(2 * half, 2 * half + 2)
                    eng.wait_ge(dt_ok, q * 2 + half + 1)
                    eng.wait_ge(u_ok, q + 1)
                    eng.tensor_tensor(dtu[p][:, cc, :], dt[p][:, cc, :], u[p][:, cc, :], ALU.mult).then_inc(dtu_ok, 1)

                def period(q, p, front, scan, end):
                    s, f, ps_ = q - 1, q - 2, 1 - p
                    for n in range(NST):
                        if scan:
                            if n == 0:
                                eng.wait_ge(dtu_ok, s * 2 + 2)
                            dbu(s, ps_, n)
                        if end and n == OUT + 2:
                            eng.wait_ge(t_ok, f + 1)
                            eng.wait_ge(g_ok, f + 1)
                            eng.wait_ge(old_in, f * 16 + 16)
                            eng.tensor_tensor(res[:, :, :], res[:, :, :], gate[:, :, :], ALU.mult).then_inc(tg_ok, 1)
                        if end and n == OUT + 3:
                            eng.wait_ge(tg_ok, f + 1)
                            eng.tensor_tensor(res[:, :, :], res[:, :, :], x_old[:, :, :], ALU.add).then_inc(res_ok, 1)
                        if front and n in (DT0 + 2, DT0 + 3):
                            step_size(q, p, n - DT0 - 2)
                        if front and n in (DT0 + 4, DT0 + 5):
                            step_input(q, p, n - DT0 - 4)

                periods(eng, period)

            @block.scalar
            def _(eng):
                def copy_b(s, n):
                    g = s * NST + n
                    eng.wait_ge(b_pe, g + 1)
                    wait(eng, dbu_ok, g - 1)
                    eng.activation(bs[n % 2][:, :], p_b[:, :], ACT.Copy).then_inc(bs_ok, 1)

                def exps(s, ps_, n):
                    g = s * NST + n
                    if n == 0:
                        eng.wait_ge(dt_ok, s * 2 + 2)
                    wait(eng, scan_ok, g - 1)
                    for c in range(CB):
                        i = eng.activation(dA[n % 2][:, c, :], dt[ps_][:, c, :], ACT.Exp, scale=a_neg[:, c, n:n + 1])
                    i.then_inc(dA_ok, 1)

                def piece(q, p, front, scan, end, n):
                    s, f, ps_ = q - 1, q - 2, 1 - p
                    if front and n == TR - 2:
                        eng.wait_ge(aggr_ok, q + 1)
                        eng.activation(std[:, :], mv[:, :, 1], ACT.Sqrt, bias=eps[:, 0:1]).then_inc(std_ok, 1)
                    if front and n == TR:
                        eng.wait_ge(tr_ok, q + 1)
                        if end:
                            eng.wait_ge(gu_pe, f * FB + FB)
                        for k in range(KD):
                            i = eng.activation(xnT[p][:, k, :], p_w[k][:, :], ACT.Copy)
                        i.then_inc(xnT_ok, 1)
                    if front and n in (XC0, XC1):
                        h = n - XC0
                        eng.wait_ge(xc_pe, q * 2 + h + 1)
                        eng.wait_ge(carry_ok, q + 1)
                        for c in two:
                            o = 2 * h + c
                            i = eng.activation(xc[:, o, 3:TT + 3], p_w[c][:, :], ACT.Identity, bias=b_in[:, o:o + 1])
                        i.then_inc(xc_ok, 1)
                    if scan and n in (Z0, Z1):
                        h = n - Z0
                        eng.wait_ge(z_pe, s * 2 + h + 1)
                        if end:
                            eng.wait_ge(yg_ok, f + 1)
                        for c in two:
                            o = 2 * h + c
                            i = eng.activation(sz[:, o, :], p_w[c][:, :], ACT.Silu, bias=b_in[:, CB + o:CB + o + 1])
                        i.then_inc(z_ok, 1)
                    if front and n == Z1:
                        eng.wait_ge(conv_ok, q * 8 + 8)
                        eng.activation(u[p][:, :, :], u[p][:, :, :], ACT.Silu).then_inc(u_ok, 1)
                    if front and n == XD:
                        eng.wait_ge(xd_pe, q + 1)
                        wait(eng, stk_ok, q)
                        eng.activation(bc[:, :], p_w[0][0:NX - RK, :], ACT.Copy)
                        eng.activation(low[NX - RK:NX, :], p_w[0][NX - RK:NX, :], ACT.Copy)
                        if end:
                            eng.wait_ge(c_pe, f * NST + NST)
                        eng.activation(stk[p][:, :], p_w[0][0:NX - RK, :], ACT.Copy).then_inc(hi_ok, 1)
                    if front and n == XD + 2:
                        eng.wait_ge(r1_ok, q + 1)
                        eng.activation(mid[:, :], bc[:, :], ACT.Copy).then_inc(mid_ok, 1)
                    if front and n in (DT0, DT1):
                        h = n - DT0
                        k2 = q * 2 + h
                        eng.wait_ge(dt_pe, k2 + 1)
                        if end and h == 0:
                            eng.wait_ge(dbu_ok, f * NST + NST)
                        cc = slice(2 * h, 2 * h + 2)
                        for c in two:
                            o = 2 * h + c
                            eng.activation(dtu[p][:, o, :], p_w[c][:, :], ACT.Relu, bias=dt_b[:, o:o + 1])
                            i = eng.activation(dt[p][:, o, :], p_w[c][:, :], ACT.Abs, bias=dt_b[:, o:o + 1])
                        i.then_inc(abs_ok, 1)
                        eng.wait_ge(abs_ok, k2 + 1)
                        eng.activation(dt[p][:, cc, :], dt[p][:, cc, :], ACT.Exp, scale=-1.0).then_inc(exp_ok, 1)
                        eng.wait_ge(exp_ok, k2 + 1)
                        eng.activation(dt[p][:, cc, :], dt[p][:, cc, :], ACT.Ln, bias=1.0).then_inc(ln_ok, 1)
                    if scan and n in GU:
                        i6 = s * FB + GU.index(n)
                        eng.wait_ge(gu_pe, i6 + 1)
                        wait(eng, h_ok, i6)
                        eng.activation(sg[:, :], p_w[0][:, :], ACT.Silu, scale=1.0 / 127.0).then_inc(sg_ok, 1)
                    if end and n == DN:
                        eng.wait_ge(dn_pe, f + 1)
                        wait(eng, tg_ok, f)
                        for h in two:
                            i = eng.activation(gate[:, 2 * h:2 * h + 2, :], p_w[h][:, :].rearrange("p (a d) -> p a d", a=2),
                                               ACT.Silu, scale=1.0 / 127.0)
                        i.then_inc(g_ok, 1)

                def period(q, p, front, scan, end):
                    s, ps_ = q - 1, 1 - p
                    for n in range(NST):
                        if scan and n < NST - 3:
                            copy_b(s, n + 3)
                        if front and n >= NST - 3:
                            copy_b(q, n - (NST - 3))
                        if scan and n < NST - 2:
                            exps(s, ps_, n + 2)
                        if front and n >= NST - 2:
                            exps(q, p, n - (NST - 2))
                        piece(q, p, front, scan, end, n)

                periods(eng, period)

            @block.tensor
            def _(eng):
                def spread(stage, psum, row, ok):
                    eng.matmul(psum[:, :], pick[:, row:row + 1].broadcast_to([3 * 2 * NST, P]), stk[stage][:, :],
                               start=True, stop=True).then_inc(ok, 1)

                def b_row(s, ps_, n):
                    g = s * NST + n
                    wait(eng, bs_ok, g)
                    if n == 0:
                        eng.wait_ge(stk_ok, s + 1)
                    spread(ps_, p_b, n, b_pe)

                def c_row(s, ps_, n):
                    wait(eng, prod_ok, s * NST + n)
                    spread(ps_, p_c, NST + n, c_pe)

                def sums(s, ps_, n):
                    g = s * NST + n
                    eng.wait_ge(prod_ok, g + 1)
                    if n == 0:
                        wait(eng, yd_ok, s)
                    for c in range(CB):
                        i = eng.matmul(p_y[:, c, :], ident[:, :], st[n % RINGS][:, c, :], start=n == 0, stop=n == NST - 1)
                    i.then_inc(y_pe, 1)

                def pair(out_of, lhs, rhs, blocks):
                    for c in two:
                        for k in range(blocks):
                            i = eng.matmul(p_w[c][:, :], lhs(c, k), rhs(k), start=k == 0, stop=k == blocks - 1)
                    i.then_inc(out_of, 1)

                def piece(q, p, front, scan, end, n):
                    s, f, ps_ = q - 1, q - 2, 1 - p
                    if front and n == TR:
                        if end:
                            eng.wait_ge(t_ok, f + 1)
                        elif scan:
                            eng.wait_ge(abs_ok, 2)
                        eng.wait_ge(xn_ok, q + 1)
                        for k in range(KD):
                            for a in range(4):
                                i = eng.transpose(p_w[k][:, a * P:(a + 1) * P], xn[:, a, k * P:(k + 1) * P], ident[:, :])
                        i.then_inc(tr_ok, 1)
                    if end and n == OUT:
                        eng.wait_ge(g_ok, f + 1)
                        eng.wait_ge(yg_ok, f + 1)
                        for a in range(4):
                            for c in range(CB):
                                i = eng.matmul(p_w[a // 2][:, (a % 2) * D:(a % 2 + 1) * D], u[p][:, c, a * P:(a + 1) * P],
                                               w_out[:, c, :], start=c == 0, stop=c == CB - 1)
                        i.then_inc(op_pe, 1)
                    if front and n in (XC0, XC1):
                        h = n - XC0
                        if h:
                            eng.wait_ge(xc_ok, q * 2 + 1)
                        else:
                            eng.wait_ge(xnT_ok, q + 1)
                        pair(xc_pe, lambda c, k: w_in[:, k, (2 * h + c) * P:(2 * h + c + 1) * P], lambda k: xnT[p][:, k, :], KD)
                    if scan and n in (Z0, Z1):
                        h = n - Z0
                        if h:
                            eng.wait_ge(z_ok, s * 2 + 1)
                        elif front:
                            eng.wait_ge(xc_ok, q * 2 + 2)
                        else:
                            eng.wait_ge(t_ok, f + 1)
                        pair(z_pe, lambda c, k: w_in[:, k, DI + (2 * h + c) * P:DI + (2 * h + c + 1) * P],
                             lambda k: xnT[ps_][:, k, :], KD)
                    if front and n == XD:
                        if scan:
                            eng.wait_ge(h_ok, s * FB + 1)
                        eng.wait_ge(u_ok, q + 1)
                        for c in range(CB):
                            i = eng.matmul(p_w[0][0:NX, :], w_x[:, c, :], u[p][:, c, :], start=c == 0, stop=c == CB - 1)
                        i.then_inc(xd_pe, 1)
                    if front and n in (DT0, DT1):
                        h = n - DT0
                        if h:
                            eng.wait_ge(abs_ok, q * 2 + 1)
                        else:
                            eng.wait_ge(hi_ok, q + 1)
                            if scan:
                                eng.wait_ge(h_ok, s * FB + 2)
                        pair(dt_pe, lambda c, k: w_dt[NX - RK:NX, (2 * h + c) * P:(2 * h + c + 1) * P],
                             lambda k: low[NX - RK:NX, :], 1)
                    if scan and n in GU:
                        i = GU.index(n)
                        if i == 0:
                            eng.wait_ge(z_ok, s * 2 + 2)
                        elif i == 1 and front:
                            eng.wait_ge(hi_ok, q + 1)
                        elif i == 2 and front:
                            eng.wait_ge(abs_ok, q * 2 + 2)
                        else:
                            eng.wait_ge(h_ok, s * FB + i)
                        pair(gu_pe, lambda c, k: (w_g, w_u)[c][:, k, i * P:(i + 1) * P], lambda k: xnT[ps_][:, k, :], KD)
                    if end and n == DN:
                        eng.wait_ge(h_ok, f * FB + FB)
                        for a in range(4):
                            for k in range(FB):
                                i = eng.matmul(p_w[a // 2][:, (a % 2) * D:(a % 2 + 1) * D], hT[:, k, a * P:(a + 1) * P],
                                               w_d[:, k, :], start=k == 0, stop=k == FB - 1)
                        i.then_inc(dn_pe, 1)

                def period(q, p, front, scan, end):
                    s, f, ps_ = q - 1, q - 2, 1 - p
                    for n in range(NST):
                        if scan and n < NST - 3:
                            b_row(s, ps_, n + 3)
                        if front and n >= NST - 3:
                            b_row(q, p, n - (NST - 3))
                        if scan:
                            if n == 0 and end:
                                sums_last(f, p)
                            c_row(s, ps_, n)
                            if n:
                                sums(s, ps_, n - 1)
                        elif n == 0 and end:
                            sums_last(f, p)
                        piece(q, p, front, scan, end, n)

                def sums_last(f, p):
                    sums(f, p, NST - 1)

                periods(eng, period)


def build_program(nc, ins, out):
    nc.disable_value_cache = True
    scratch = lambda name, shape, d=F32: nc.dram_tensor("s_" + name, shape, d).ap()
    scr = {
        "kp": scratch("kp", (NT * HG * 48, 4 * TT), BF16),
        "vp": scratch("vp", (NT * HG, P, 4 * 4 * VW)),
        "lg": scratch("lg", (NT * NE, TT)),
        "qp": scratch("qp", (B * HG, 3 * 64, SB), BF16).rearrange("(b a) z t -> b a z t", b=B),
        "rows": scratch("rows", (P, TOPK)),
        "oe": scratch("oe", (B, NE, D)),
        "x1": scratch("x1", (B * S, D)),
        "out": out,
    }
    tokens_stage(nc, ins, scr)
    with ExitStack() as ctx:
        keep = {n: ctx.enter_context(nc.sbuf_tensor("keep_" + n, s, F32)) for n, s in (
            ("ident", [P, P]), ("xg", [P, TOPK, D]), ("vals", [P, TOPK]), ("gf", [P, TOPK]),
            ("mergedT", [P, NE, KD, B]), ("accT", [P, HG, TOPK, B, NE]))}
        routing_stage(nc, ins, scr, keep)
        attention_stage(nc, ins, scr, keep)
        scatter_stage(nc, ins, scr, keep)
    layer1_stage(nc, ins, scr)


def lay_out(inputs):
    f = lambda n: np.ascontiguousarray(np.asarray(inputs[n]))
    cont = np.ascontiguousarray
    z = {"x": f("L0_attn_x").reshape(B * S, D), "ident": np.eye(P, dtype=np.float32)}

    hg, j, hh = np.meshgrid(np.arange(HG), np.arange(HD // 2), np.arange(4), indexing="ij")
    pairs = ((hg * 4 + hh) * (HD // 2) + j).reshape(-1)
    cols = np.concatenate([2 * pairs, 2 * pairs + 1])
    for name in ("Wk_r", "Wu_k", "Wq_r", "Wu_q"):
        z[name] = cont(f(f"L0_attn_{name}_w")[:, cols])
    z["b_kr"] = cont(f("L0_attn_Wk_r_b")[cols].reshape(2, P).T)
    z["b_uk"] = cont(f("L0_attn_Wu_k_b")[cols].reshape(2, P).T)
    z["b_qr"], z["b_uq"] = f("L0_attn_Wq_r_b")[cols], f("L0_attn_Wu_q_b")[cols]

    theta = np.float32(10000.0) ** (np.float32(-2.0) * np.arange(D // 2, dtype=np.float32)) / np.float32(D // 2)
    angle = (np.arange(S, dtype=np.float32)[:, None] * theta[None, :]).astype(np.float32)
    cos, sin = np.cos(angle).astype(np.float32)[:, pairs], np.sin(angle).astype(np.float32)[:, pairs]
    z["cs_rows"] = cont(np.concatenate([cos, sin], 1))
    tiles = np.stack([cos.T, sin.T], 1).reshape(P, 2, NC, TT).transpose(2, 0, 1, 3)
    z["cs_tiles"] = cont(np.concatenate([tiles] * B, 0).reshape(NT * P, 2, TT))

    z["Wd_kv"], z["Wd_q"] = f("L0_attn_Wd_kv_w"), f("L0_attn_Wd_q_w")
    z["Wu_v"], z["b_uv"], z["Wo"], z["b_o"] = (f("L0_attn_" + n) for n in ("Wu_v_w", "Wu_v_b", "Wo_w", "Wo_b"))
    z["gateT"] = cont(f("L0_ffn_gate_w").T)
    z["b_dkv"], z["b_dq"] = f("L0_attn_Wd_kv_b").reshape(P, 1), f("L0_attn_Wd_q_b").reshape(P, 1)
    z["b_gate"] = f("L0_ffn_gate_b").reshape(NE, 1)
    z["first"] = np.repeat(np.arange(B) * S, NE).astype(np.float32).reshape(P, 1)
    z["rank"] = (NS - np.arange(NS)).astype(np.float32).reshape(P, TOPK)
    z["w1"], z["w2"] = f("L0_ffn_w1"), f("L0_ffn_w2")
    z["b1T"] = cont(z["w1"][:, D, :].reshape(NE, HID // P, P).transpose(2, 0, 1))
    z["b2"] = cont(z["w2"][:, HID, :])

    g = lambda n: f("L1_" + n)
    z["fc1_w"], z["fc1_b"] = g("attn_fc1_w"), cont(g("attn_fc1_b").reshape(KD, P).T)
    z["in_projT"], z["out_proj_w"] = cont(g("attn_in_proj_w").T), g("attn_out_proj_w")
    z["fc2_wT"], z["fc2_b"] = cont(g("attn_fc2_w").T), g("attn_fc2_b")
    z["wgT"], z["wuT"], z["wdT"] = (cont(g("ffn_" + n).T) for n in ("w_gate", "w_up", "w_down"))
    z["pick"] = np.tile(np.eye(2 * NST, dtype=np.float32), (3, 1))
    z["A_log"], z["conv_w"] = g("attn_A_log"), g("attn_conv_w")
    xp = g("attn_x_proj_w")
    z["x_projT"] = cont(np.concatenate([xp[RK:], xp[RK:], xp[RK:], xp[:RK]], 0).T)
    z["dt_projT"] = cont(g("attn_dt_proj_w").T)
    for name, source in (("conv_b", "attn_conv_b"), ("skip", "attn_D"), ("dt_b", "attn_dt_proj_b")):
        z[name] = cont(g(source).reshape(CB, P).T)
    z["mask"] = np.ones((P, NT + 1), np.float32)
    z["mask"][:, ::NC] = 0
    return z


def kernel(**inputs):
    import concourse.bacc as bacc
    from concourse.bass_utils import run_bass_kernel_spmd

    nc = bacc.Bacc("TRN2", target_bir_lowering=False, num_devices=1)
    arrays, ins = {}, {}
    for name, a in lay_out(inputs).items():
        arrays[f"in_{name}_dram"] = a
        ins[name] = nc.dram_tensor(f"in_{name}_dram", a.shape, mybir.dt.from_np(a.dtype), kind="ExternalInput").ap()
    out = nc.dram_tensor("out_0_dram", (B * S, D), F32, kind="ExternalOutput").ap()
    build_program(nc, ins, out)
    r = run_bass_kernel_spmd(nc, [arrays], core_ids=[0])
    return r.results[0]["out_0_dram"].reshape(B, S, D)
```
